# Optimizing a Trainium2 kernel written in Bass

```python
import numpy as np
import jax
import jax.numpy as jnp

def _softmax(x, axis=-1):
    return jax.nn.softmax(x, axis=axis)

def _gelu(x):
    return jax.nn.gelu(x, approximate=True)

def _silu(x):
    return jax.nn.silu(x)

def _sigmoid(x):
    return jax.nn.sigmoid(x)

def _layernorm(x, axis=-1, eps=1e-05):
    m = jnp.mean(x, axis=axis, keepdims=True)
    v = jnp.var(x, axis=axis, keepdims=True)
    return (x - m) / jnp.sqrt(v + eps)

def _scatter_add(tgt, idx, src, axis=0):
    return tgt.at[idx].add(src)

def _segment_sum(src, seg, n):
    return jax.ops.segment_sum(src, seg, n)
kernel_name = 'mk_seq_preln_d1_jaxref_r4_6a69b6'

def setup_inputs(seed: int=0):
    np.random.seed(seed)
    _w = jnp.asarray

    def _L0_attn_setup():
        import jax, jax.numpy as jnp
        import numpy as np
        H = 16
        EPS_DEN = 1e-06

        def _decay_scan(x, decay, init):
            xT = jnp.moveaxis(x, 2, 0)

            def step(s, xt):
                s = decay * s + xt
                return (s, s)
            _, ys = jax.lax.scan(step, init, xT)
            return jnp.moveaxis(ys, 0, 2)

        def _phi(z):
            return jax.nn.elu(z) + 1.0

        def _reference_tuple_inner(x, w_qkv, w_out, decay_param):
            B, T, Hid = x.shape
            D = Hid // H
            qkv = x @ w_qkv
            q, k, v = jnp.split(qkv, 3, axis=-1)

            def to_bhtd(t):
                return t.reshape(B, T, H, D).transpose(0, 2, 1, 3)
            q = _phi(to_bhtd(q))
            k = _phi(to_bhtd(k))
            v = to_bhtd(v)
            decay = jax.nn.sigmoid(decay_param).reshape(1, H, 1)
            init = jnp.zeros((B, H, D), dtype=x.dtype)
            running_kv = _decay_scan(k * v, decay, init)
            running_ksum = _decay_scan(k, decay, init)
            den = jnp.clip(jnp.sum(q * running_ksum, axis=-1, keepdims=True), EPS_DEN, None)
            out = q * running_kv / den
            out = out.transpose(0, 2, 1, 3).reshape(B, T, Hid) @ w_out
            new_kv = running_kv[:, :, -1, :]
            new_ksum = running_ksum[:, :, -1, :]
            return (out, new_kv, new_ksum)
        key = jax.random.key(seed)
        k1, k2, k3 = jax.random.split(key, 3)
        x = jax.random.normal(k1, (2, 1024, 512), dtype=jnp.float32)
        w_qkv = jax.random.normal(k2, (512, 1536), dtype=jnp.float32) * 0.02
        w_out = jax.random.normal(k3, (512, 512), dtype=jnp.float32) * 0.02
        decay_param = jnp.full((H,), 0.95, dtype=jnp.float32)
        return {'x': x, 'w_qkv': w_qkv, 'w_out': w_out, 'decay_param': decay_param}
    _L0_attn_in = _L0_attn_setup()

    def _L0_ffn_setup():
        import jax, jax.numpy as jnp
        import numpy as np
        B, S, D = (4, 128, 512)
        E, K, H = (8, 2, 352)
        HS = 2 * 352
        ALPHA = 0.001
        W_SCALE = 0.02

        def _moe_forward(hidden_states, gate_w, w_gate, w_up, w_down, sw_gate, sw_up, sw_down):
            b, s, d = hidden_states.shape
            x = hidden_states.reshape(-1, d)
            T = x.shape[0]
            logits = x @ gate_w
            scores = jax.nn.softmax(logits, axis=-1)
            topk_w, topk_idx = jax.lax.top_k(scores, K)
            mask = jax.nn.one_hot(topk_idx, E, dtype=scores.dtype).sum(axis=1)
            ce = mask.mean(axis=0)
            Pi = scores.mean(axis=0)
            aux_loss = (Pi * ce * E).sum() * ALPHA
            comb = jnp.zeros((T, E), dtype=x.dtype)
            comb = comb.at[jnp.arange(T)[:, None], topk_idx].add(topk_w)
            g = jax.nn.silu(jnp.einsum('td,edh->teh', x, w_gate)) * jnp.einsum('td,edh->teh', x, w_up)
            routed = jnp.einsum('teh,ehd,te->td', g, w_down, comb)
            shared = jax.nn.silu(x @ sw_gate) * (x @ sw_up) @ sw_down
            out = (routed + shared).reshape(b, s, d)
            return (out, aux_loss)
        key = jax.random.key(seed)
        ks = jax.random.split(key, 8)
        rn = lambda k, sh: jax.random.normal(k, sh, dtype=jnp.float32)
        return {'hidden_states': rn(ks[0], (B, S, D)), 'gate_w': rn(ks[1], (D, E)) * W_SCALE, 'w_gate': rn(ks[2], (E, D, H)) * W_SCALE, 'w_up': rn(ks[3], (E, D, H)) * W_SCALE, 'w_down': rn(ks[4], (E, H, D)) * W_SCALE, 'sw_gate': rn(ks[5], (D, HS)) * W_SCALE, 'sw_up': rn(ks[6], (D, HS)) * W_SCALE, 'sw_down': rn(ks[7], (HS, D)) * W_SCALE}
    _L0_ffn_in = _L0_ffn_setup()
    _d = {'L0_attn_x': _L0_attn_in['x'], 'L0_attn_w_qkv': _L0_attn_in['w_qkv'], 'L0_attn_w_out': _L0_attn_in['w_out'], 'L0_attn_decay_param': _L0_attn_in['decay_param'], 'L0_ffn_gate_w': _L0_ffn_in['gate_w'], 'L0_ffn_w_gate': _L0_ffn_in['w_gate'], 'L0_ffn_w_up': _L0_ffn_in['w_up'], 'L0_ffn_w_down': _L0_ffn_in['w_down'], 'L0_ffn_sw_gate': _L0_ffn_in['sw_gate'], 'L0_ffn_sw_up': _L0_ffn_in['sw_up'], 'L0_ffn_sw_down': _L0_ffn_in['sw_down']}
    _x0 = _d['L0_attn_x']
    _d['L0_attn_x'] = jax.random.normal(jax.random.fold_in(jax.random.key(seed), 1), (2, 1024, 512), dtype=_x0.dtype)
    del _x0
    return _d

def reference(L0_attn_x, L0_attn_w_qkv, L0_attn_w_out, L0_attn_decay_param, L0_ffn_gate_w, L0_ffn_w_gate, L0_ffn_w_up, L0_ffn_w_down, L0_ffn_sw_gate, L0_ffn_sw_up, L0_ffn_sw_down):

    def _L0_attn_ref(x, w_qkv, w_out, decay_param):
        import jax, jax.numpy as jnp
        import numpy as np
        H = 16
        EPS_DEN = 1e-06

        def _decay_scan(x, decay, init):
            xT = jnp.moveaxis(x, 2, 0)

            def step(s, xt):
                s = decay * s + xt
                return (s, s)
            _, ys = jax.lax.scan(step, init, xT)
            return jnp.moveaxis(ys, 0, 2)

        def _phi(z):
            return jax.nn.elu(z) + 1.0

        def _reference_tuple_inner(x, w_qkv, w_out, decay_param):
            B, T, Hid = x.shape
            D = Hid // H
            qkv = x @ w_qkv
            q, k, v = jnp.split(qkv, 3, axis=-1)

            def to_bhtd(t):
                return t.reshape(B, T, H, D).transpose(0, 2, 1, 3)
            q = _phi(to_bhtd(q))
            k = _phi(to_bhtd(k))
            v = to_bhtd(v)
            decay = jax.nn.sigmoid(decay_param).reshape(1, H, 1)
            init = jnp.zeros((B, H, D), dtype=x.dtype)
            running_kv = _decay_scan(k * v, decay, init)
            running_ksum = _decay_scan(k, decay, init)
            den = jnp.clip(jnp.sum(q * running_ksum, axis=-1, keepdims=True), EPS_DEN, None)
            out = q * running_kv / den
            out = out.transpose(0, 2, 1, 3).reshape(B, T, Hid) @ w_out
            new_kv = running_kv[:, :, -1, :]
            new_ksum = running_ksum[:, :, -1, :]
            return (out, new_kv, new_ksum)
        return _reference_tuple_inner(x, w_qkv, w_out, decay_param)[0]

    def _L0_ffn_ref(hidden_states, gate_w, w_gate, w_up, w_down, sw_gate, sw_up, sw_down):
        import jax, jax.numpy as jnp
        import numpy as np
        B, S, D = (4, 128, 512)
        E, K, H = (8, 2, 352)
        HS = 2 * 352
        ALPHA = 0.001
        W_SCALE = 0.02

        def _moe_forward(hidden_states, gate_w, w_gate, w_up, w_down, sw_gate, sw_up, sw_down):
            b, s, d = hidden_states.shape
            x = hidden_states.reshape(-1, d)
            T = x.shape[0]
            logits = x @ gate_w
            scores = jax.nn.softmax(logits, axis=-1)
            topk_w, topk_idx = jax.lax.top_k(scores, K)
            mask = jax.nn.one_hot(topk_idx, E, dtype=scores.dtype).sum(axis=1)
            ce = mask.mean(axis=0)
            Pi = scores.mean(axis=0)
            aux_loss = (Pi * ce * E).sum() * ALPHA
            comb = jnp.zeros((T, E), dtype=x.dtype)
            comb = comb.at[jnp.arange(T)[:, None], topk_idx].add(topk_w)
            g = jax.nn.silu(jnp.einsum('td,edh->teh', x, w_gate)) * jnp.einsum('td,edh->teh', x, w_up)
            routed = jnp.einsum('teh,ehd,te->td', g, w_down, comb)
            shared = jax.nn.silu(x @ sw_gate) * (x @ sw_up) @ sw_down
            out = (routed + shared).reshape(b, s, d)
            return (out, aux_loss)
        out, _aux = _moe_forward(hidden_states, gate_w, w_gate, w_up, w_down, sw_gate, sw_up, sw_down)
        return out
    x = L0_attn_x
    x = x + _L0_attn_ref(_layernorm(x, axis=-1), L0_attn_w_qkv, L0_attn_w_out, L0_attn_decay_param)
    x = x + _L0_ffn_ref(_layernorm(x, axis=-1), L0_ffn_gate_w, L0_ffn_w_gate, L0_ffn_w_up, L0_ffn_w_down, L0_ffn_sw_gate, L0_ffn_sw_up, L0_ffn_sw_down)
    return x

_drawn_inputs = setup_inputs


def setup_inputs(seed=0):
    import zlib

    import numpy as np

    out = dict(_drawn_inputs(seed))
    spreads = {'L0_attn_decay_param': (0.949999988079071, 0.6)}
    factors = {'L0_attn_w_qkv': 8.0,
     'L0_attn_w_out': 8.0,
     'L0_ffn_gate_w': 5.564,
     'L0_ffn_w_gate': 4.946,
     'L0_ffn_w_up': 4.835,
     'L0_ffn_w_down': 4.827,
     'L0_ffn_sw_gate': 4.404,
     'L0_ffn_sw_up': 4.309,
     'L0_ffn_sw_down': 4.312}
    for name, (base, spread) in spreads.items():
        noise = np.random.default_rng([zlib.crc32(name.encode()), seed]).standard_normal(out[name].shape)
        drawn = base * np.exp(spread * noise) if base else spread * noise
        out[name] = jnp.asarray(drawn.astype(out[name].dtype))
    for name, factor in factors.items():
        out[name] = (out[name] * factor).astype(out[name].dtype)
    return out
```

```python
from contextlib import ExitStack

import concourse.bass as bass
from concourse import mybir

P = 128
F32 = mybir.dt.float32
F32R = mybir.dt.float32r
I32 = mybir.dt.int32
U32 = mybir.dt.uint32
ALU = mybir.AluOpType
ACT = mybir.ActivationFunctionType
AX_X = mybir.AxisListType.X

LN_EPS = 1e-5
DEN_EPS = 1e-6


def preln_decay_attention_moe(nc, x, w_qkv, w_out, decay, gate_w, w_gate, w_up, w_down,
                              sw_gate, sw_up, sw_down, out):
    B, S, D = x.shape
    T = B * S
    HEADS = decay.shape[0]
    DH = D // HEADS
    E, _, F = w_gate.shape
    KC = D // P
    NT = T // P
    BLK = 512
    TPB = BLK // P
    NB = T // BLK
    BPS = S // BLK
    HALVES = sw_gate.shape[1] // F
    assert HALVES == 2 and NT % 4 == 0 and D == BLK
    FROWS = [min(P, F - P * c) for c in range((F + P - 1) // P)]
    FC = len(FROWS)
    TOPK = 2
    JOBS = (TOPK * T - E) // P + E
    JOBS -= 1 if (TOPK * T + E * (P - 1)) // P < JOBS else 0
    JW = JOBS + JOBS % 2
    ROWS = T + P

    xf = x.rearrange("b s d -> (b s) d")
    xn2_d = nc.dram_tensor("xn2_scratch", [ROWS, D], F32, kind="Internal").ap()

    with ExitStack() as ctx:
        def sb(name, shape, dt=F32, stack=ctx):
            return stack.enter_context(nc.sbuf_tensor(name, shape, dt))

        def psum(name, shape, dt=F32, stack=ctx):
            return stack.enter_context(nc.psum_tensor(name, shape, dt))

        def sem(name):
            return ctx.enter_context(nc.semaphore(name))

        ident = sb("ident", [P, P])
        gw = sb("gw", [P, KC, E])
        logits = sb("logits", [P, NT, E])
        attn = ExitStack()
        asb = lambda name, shape, dt=F32: sb(name, shape, dt, attn)
        wq_h = asb("wq_h", [P, KC, 3 * D], F32R)
        wq_l = asb("wq_l", [P, KC, 3 * D], F32R)
        wo_h = asb("wo_h", [P, KC, D], F32R)
        wo_l = asb("wo_l", [P, KC, D], F32R)
        w_raw = asb("w_raw", [P, 3 * D])
        head_of = asb("head_of", [P, KC, HEADS])
        of_head = asb("of_head", [HEADS, KC, P])
        dec = asb("dec", [P, KC])
        carry = asb("carry", [P, 2, KC])
        x_in = asb("x_in", [P, 2, D])
        x_res = asb("x_res", [P, 2, D])
        stats = asb("stats", [P, 2, 6])
        mean_var = asb("mean_var", [P, 2, 2])
        var_eps = asb("var_eps", [P, 2])
        rstd = asb("rstd", [P, 2])
        stats2 = asb("stats2", [P, 6])
        mean_var2 = asb("mean_var2", [P, 2])
        var_eps2 = asb("var_eps2", [P, 1])
        rstd2 = asb("rstd2", [P, 1])
        neg_half = asb("neg_half", [P, 1])
        xn = asb("xn", [P, D])
        xnT_h = asb("xnT_h", [P, 2, KC, BLK], F32R)
        xnT_l = asb("xnT_l", [P, 2, KC, BLK], F32R)
        exp_z = asb("exp_z", [P, 2, BLK])
        relu_z = asb("relu_z", [P, 2, BLK])
        phi_k = asb("phi_k", [P, BLK])
        phi_q = asb("phi_q", [P, BLK])
        kv = asb("kv", [P, BLK])
        run_k = asb("run_k", [P, BLK])
        run_kv = asb("run_kv", [P, BLK])
        qk = asb("qk", [P, 2, BLK])
        num = asb("num", [P, 2, KC, BLK])
        den = asb("den", [HEADS, BLK])
        rden = asb("rden", [HEADS, BLK])
        at_h = asb("at_h", [P, KC, BLK], F32R)
        at_l = asb("at_l", [P, KC, BLK], F32R)
        x2 = asb("x2", [P, D])
        xn2 = asb("xn2", [P, D])
        xn2T = asb("xn2T", [P, KC, P])
        attn.close()
        moe = ExitStack()
        msb = lambda name, shape, dt=F32: sb(name, shape, dt, moe)
        wg = msb("wg", [P, E, KC, F])
        wu = msb("wu", [P, E, KC, F])
        wd = msb("wd", [P, E, FC, D])
        x_job = msb("x_job", [P, 2, D])
        xT = msb("xT", [P, 2, KC, P])
        silu = msb("silu", [P, 2, F])
        hid = msb("hid", [P, 2, F])
        hidT = msb("hidT", [P, 2, FC, P])
        y_job = msb("y_job", [P, 2, D])
        sg = msb("sg", [P, KC, HALVES * F])
        su = msb("su", [P, KC, HALVES * F])
        sd = msb("sd", [P, HALVES, FC, D])
        tri = msb("tri", [P, P])
        ones = msb("ones", [P, P])
        zeros = msb("zeros", [P, D // 8])
        iota_e = msb("iota_e", [P, E])
        iota_j = msb("iota_j", [P, JW])
        iota_p = msb("iota_p", [P, P])
        token_1 = msb("token_1", [P, NT])
        spare = msb("spare", [P, 1])
        not_first = msb("not_first", [P, E, NT])
        row_a = msb("row_a", [P, NT])
        row_b = msb("row_b", [P, NT])
        tab_a = msb("tab_a", [P, NT, E])
        score = msb("score", [P, NT, E])
        top = msb("top", [P, NT, 8])
        top_i = msb("top_i", [P, NT, 8], U32)
        top_f = msb("top_f", [P, TOPK, NT])
        pick = msb("pick", [P, TOPK, NT, E])
        picked = msb("picked", [P, NT, E])
        count = msb("count", [P, E, NT])
        upto = msb("upto", [P, E, NT])
        base = msb("base", [P, E, NT])
        slot_e = msb("slot_e", [P, NT, E])
        jobs_f = msb("jobs_f", [P, E])
        jobs_i = msb("jobs_i", [P, E], I32)
        jobs_end = msb("jobs_end", [P, E])
        jobs_beg = msb("jobs_beg", [P, E])
        slot_f = msb("slot_f", [P, TOPK, NT])
        slot_i = msb("slot_i", [P, TOPK * NT], I32)
        slot_ji = msb("slot_ji", [P, TOPK * NT], I32)
        slot_pi = msb("slot_pi", [P, TOPK * NT], I32)
        slot_j = msb("slot_j", [P, TOPK * NT])
        slot_p = msb("slot_p", [P, TOPK * NT])
        hot_p = msb("hot_p", [P, 2, P])
        hot_j = msb("hot_j", [P, 2, 2, JW])
        past = msb("past", [P, JW, E])
        job_ef = msb("job_ef", [P, JW])
        job_e = msb("job_e", [P, JW], I32)
        job_tok1 = msb("job_tok1", [P, JW])
        job_pad = msb("job_pad", [P, JW])
        job_tok = msb("job_tok", [P, JW], I32)
        job_w = msb("job_w", [P, JW])
        idx_in = msb("idx_in", [P, 2], I32)
        idx_out = msb("idx_out", [P, 2], I32)
        moe.close()

        pa = ExitStack()
        turn = psum("turn", [P, KC, P], stack=pa)
        RING = 5
        ring = [psum(f"ring{i}", [P, BLK], stack=pa) for i in range(RING)]
        ps_den = psum("ps_den", [P, BLK], stack=pa)
        ps_gate = psum("ps_gate", [P, NT, 4 * E], stack=pa)
        pa.close()
        pm = ExitStack()
        turn_x = psum("turn_x", [P, KC, P], stack=pm)
        turn_h = psum("turn_h", [P, 4, P], stack=pm)
        ps_g = [psum(f"ps_g{i}", [P, 512], stack=pm) for i in range(2)]
        ps_y = [psum(f"ps_y{i}", [P, D], stack=pm) for i in range(2)]
        ps_u = [psum(f"ps_u{i}", [P, 512], stack=pm) for i in range(2)]
        pm.close()

        names = """w_in w_out_in w_hi w_lo consts dec_in dec_e dec_1 dec_ok gw_in xl0 xl1 stat1 var1 veps1 rstd1
            xn1 turned1 hi1 lo1 k_mm v_mm q_mm k_act q_act phik_s kv_s sk_s skv_s carry_s phiq_s qk_s num_s
            den_mm den_max rden_s ex_mm a_s ah_s al_s out_mm xr0 xr1 x2_s stat2 var2 veps2 rstd2_s xn2_s
            turned2 xn2T_s gate_mm logit_s x2_out xn2_out pad_out cst_a cst_b
            shared_in routed_in d_route rt_exp rt_exp_in rank_mm picked_s hot_s acc_mm tables_s
            xin0 xin1 gin0 gin1 turned_x xT_s gu_mm silu_s hid_s turned_h hidT_s y_mm y_s idxg_s idxs_s yo0 yo1""".split()
        s = {n: sem(n) for n in names}
        block = ctx.enter_context(nc.Block())

        blocks = range(NB)
        chunks = range(KC)
        ps_rank, ps_acc = ps_g[0], ps_g[1]
        SHARED_DMAS = 2 + 2 * HALVES
        ROUTED_DMAS = 4 * E
        items = {}
        k_item = lambda n, c: items[(n, c, "k")]
        q_item = lambda n, c: items[(n, c, "q")]
        v_item = lambda n, c: items[(n, c, "v")]
        release = []

        def bank(eng, freed_by, value):
            m = len(release)
            if m >= RING:
                eng.wait_ge(*release[m - RING])
            release.append((s[freed_by], value))
            return ring[m % RING]

        tile_sem = lambda pair, t: (s[f"{pair}{t % 2}"], 16 * (t // 2 + 1))
        LAST = (NB - 1) * TPB + TPB

        @block.tensor
        def _(pe):
            def split_product(ps, pairs):
                steps = []
                for (ah, al), (bh, bl) in pairs:
                    steps += [(ah, bh), (ah, bl), (al, bh)]
                for i, (a, b) in enumerate(steps):
                    ins = pe.matmul(ps, a, b, start=(i == 0), stop=(i == len(steps) - 1))
                return ins

            def turn_x1(t):
                pe.wait_ge(s["xn1"], t + 1)
                if t:
                    pe.wait_ge(s["lo1"], t)
                for k in chunks:
                    ins = pe.transpose(turn[:, k, :], xn[:, k * P:(k + 1) * P], ident[:, :])
                ins.then_inc(s["turned1"], 1)

            def project(n, c, z):
                i = n * KC + c
                name, freed = {0: ("q", "q_act"), 1: ("k", "k_act"), 2: ("v", "kv_s")}[z]
                items[(n, c, name)] = len(release)
                ps = bank(pe, freed, i + 1)
                pairs = []
                for k in chunks:
                    cols = slice(z * D + c * P, z * D + (c + 1) * P)
                    pairs.append(((wq_h[:, k, cols], wq_l[:, k, cols]), (xnT_h[:, n % 2, k, :], xnT_l[:, n % 2, k, :])))
                split_product(ps[:, :], pairs).then_inc(s[name + "_mm"], 1)

            def sum_heads(n, c):
                i = n * KC + c
                pe.wait_ge(s["qk_s"], i + 1)
                if n and c == 0:
                    pe.wait_ge(s["den_max"], n)
                pe.matmul(ps_den[0:HEADS, :], head_of[:, c, :], qk[:, c % 2, :], start=(c == 0), stop=(c == KC - 1))\
                    .then_inc(s["den_mm"], 1)

            def expand(n):
                pe.wait_ge(s["rden_s"], n + 1)
                for c in chunks:
                    items[(n, c, "ex")] = len(release)
                    ps = bank(pe, "a_s", n * KC + c + 1)
                    pe.matmul(ps[:, :], of_head[:, c, :], rden[:, :], start=True, stop=True).then_inc(s["ex_mm"], 1)

            def output(n):
                pe.wait_ge(s["al_s"], (n + 1) * KC)
                for j in range(TPB):
                    items[(n, j, "out")] = len(release)
                    ps = bank(pe, "x2_s", n * TPB + j + 1)
                    tok = slice(j * P, (j + 1) * P)
                    split_product(ps[:, :], [((at_h[:, k, tok], at_l[:, k, tok]), (wo_h[:, k, :], wo_l[:, k, :]))
                                             for k in chunks]).then_inc(s["out_mm"], 1)

            def gate(n):
                for j in range(TPB):
                    t = n * TPB + j
                    pe.wait_ge(s["xn2_s"], t + 1)
                    if j == 0:
                        pe.wait_ge(s["lo1"], min(NT, (n + 3) * TPB))
                    if t:
                        pe.wait_ge(s["xn2T_s"], t)
                    for k in chunks:
                        ins = pe.transpose(turn[:, k, :], xn2[:, k * P:(k + 1) * P], ident[:, :])
                    ins.then_inc(s["turned2"], 1)
                    pe.wait_ge(s["xn2T_s"], t + 1)
                    for k in chunks:
                        ins = pe.matmul(ps_gate[:, t, 0:E], xn2T[:, k, :], gw[:, k, :], start=(k == 0),
                                        stop=(k == KC - 1))
                    ins.then_inc(s["gate_mm"], 1)

            pe.wait_ge(s["consts"], 1)
            for t in range(TPB):
                turn_x1(t)
            pe.wait_ge(s["w_lo"], KC)
            for n in blocks:
                pe.wait_ge(s["lo1"], (n + 1) * TPB)
                for c in chunks:
                    project(n, c, 1)
                    if n == 0 and c == 0:
                        pe.wait_ge(s["consts"], 2)
                    if c:
                        sum_heads(n, c - 1)
                    elif n:
                        sum_heads(n - 1, KC - 1)
                    project(n, c, 2)
                    project(n, c, 0)
                    if n and c == 1:
                        expand(n - 1)
                    if n + 1 < NB and c in (1, 2):
                        for j in (0, 1):
                            turn_x1((n + 1) * TPB + 2 * (c - 1) + j)
                    if n and c == 2:
                        output(n - 1)
                    if n == 1 and c == 3:
                        pe.wait_ge(s["gw_in"], 16)
                    if n and c == 3:
                        gate(n - 1)
            sum_heads(NB - 1, KC - 1)
            expand(NB - 1)
            pe.wait_ge(s["w_lo"], 2 * KC)
            output(NB - 1)
            gate(NB - 1)

            def turn_job(t, b, first=False, routed=None):
                if routed is None:
                    pe.wait_ge(s[f"xin{b}"], 8 * (t - b) + 16)
                else:
                    pe.wait_ge(s[f"gin{b}"], 8 * (routed - b) + 16)
                if not first:
                    pe.wait_ge(s["xT_s"], t)
                for k in chunks:
                    ins = pe.transpose(turn_x[:, k, :], x_job[:, b, k * P:(k + 1) * P], ident[:, :])
                ins.then_inc(s["turned_x"], 1)

            def gate_up(u, b, t, tb, w_g, w_u, first=False):
                pe.wait_ge(s["xT_s"], t + 1)
                if not first:
                    pe.wait_ge(s["hid_s"], u - 1)
                for ps, w in ((ps_g[b], w_g), (ps_u[b], w_u)):
                    for k in chunks:
                        ins = pe.matmul(ps[:, 0:F], xT[:, tb, k, :], w(k), start=(k == 0), stop=(k == KC - 1))
                ins.then_inc(s["gu_mm"], 1)

            def turn_hidden(u, b, first=False):
                pe.wait_ge(s["hid_s"], u + 1)
                if not first:
                    pe.wait_ge(s["hidT_s"], u)
                for c, rows in enumerate(FROWS):
                    ins = pe.transpose(turn_h[0:rows, c, :], hid[:, b, c * P:c * P + rows], ident[:, :])
                ins.then_inc(s["turned_h"], 1)

            def down(u, b, t, tb, w_d, start, stop, first=False):
                pe.wait_ge(s["hidT_s"], u + 1)
                if start and not first:
                    pe.wait_ge(s["y_s"], t - 1)
                for c, rows in enumerate(FROWS):
                    ins = pe.matmul(ps_y[tb][:, :], hidT[0:rows, b, c, :], w_d(c, rows),
                                    start=(start and c == 0), stop=(stop and c == FC - 1))
                if stop:
                    ins.then_inc(s["y_mm"], 1)

            def gate_up_shared(u, half, t, tb, first=False):
                cols = slice(half * F, (half + 1) * F)
                gate_up(u, half, t, tb, lambda k: sg[:, k, cols], lambda k: su[:, k, cols], first)

            def down_shared(u, half, t, tb, first=False, first_y=False):
                turn_hidden(u, half, first)
                down(u, half, t, tb, lambda c, rows: sd[0:rows, half, c, :], half == 0, half == 1, first_y)

            def gate_up_routed(r, b):
                e = pe.value_load(job_e[0:1, bass.ds(r, 1)], min_val=0, max_val=E - 1)
                gate_up(HALVES * NT + r, b, NT + r, b, lambda k: wg[:, e, k, :], lambda k: wu[:, e, k, :])
                return e

            def down_routed(r, b):
                e = pe.value_load(job_e[0:1, bass.ds(r, 1)], min_val=0, max_val=E - 1)
                u = HALVES * NT + r
                turn_hidden(u, b)
                down(u, b, NT + r, b, lambda c, rows: wd[0:rows, e, c, :], True, True)

            def rank_tokens():
                pe.wait_ge(s["picked_s"], 1)
                pe.matmul(ps_rank[:, 0:P], tri[:, :], picked[:, :, :].rearrange("p t e -> p (t e)"),
                          start=True, stop=True)
                pe.matmul(ps_rank[:, P:2 * P], ones[:, :], picked[:, :, :].rearrange("p t e -> p (t e)"),
                          start=True, stop=True).then_inc(s["rank_mm"], 1)

            def slot_tables():
                n = TOPK * NT
                for m in range(n):
                    pe.wait_ge(s["hot_s"], m + 1)
                    pe.matmul(ps_acc[:, 0:2 * JW], hot_p[:, m % 2, :], hot_j[:, m % 2].rearrange("p a j -> p (a j)"),
                              start=(m == 0), stop=(m == n - 1)).then_inc(s["acc_mm"], 1)

            pe.wait_ge(s["logit_s"], 1)
            turn_job(0, 0, True)
            pe.wait_ge(s["cst_b"], 1)
            rank_tokens()
            slot_tables()
            pe.wait_ge(s["shared_in"], 16 * SHARED_DMAS)
            pe.wait_ge(s["tables_s"], 1)
            gate_up_shared(0, 0, 0, 0, True)

            def two_tiles(i, first=False, last=False):
                u, t = 4 * i, 2 * i
                gate_up_shared(u + 1, 1, t, 0, first)
                down_shared(u, 0, t, 0, first, first)
                turn_job(t + 1, 1)
                gate_up_shared(u + 2, 0, t + 1, 1)
                down_shared(u + 1, 1, t, 0)
                gate_up_shared(u + 3, 1, t + 1, 1)
                down_shared(u + 2, 0, t + 1, 1, False, first)
                if not last:
                    turn_job(t + 2, 0)
                    gate_up_shared(u + 4, 0, t + 2, 0)
                    down_shared(u + 3, 1, t + 1, 1)

            two_tiles(0, first=True)
            with pe.Fori(1, NT // 2 - 1) as i:
                two_tiles(i)
            two_tiles(NT // 2 - 1, last=True)
            pe.wait_ge(s["routed_in"], 16 * ROUTED_DMAS)
            turn_job(NT, 0, routed=0)
            gate_up_routed(0, 0)
            down_shared(2 * NT - 1, 1, NT - 1, 1)
            with pe.Fori(0, JOBS // 2) as i:
                for b in range(2):
                    r = 2 * i + b
                    turn_job(NT + r + 1, 1 - b, routed=r + 1)
                    gate_up_routed(r + 1, 1 - b)
                    down_routed(r, b)
            down_routed(JOBS - 1, 0)

        @block.sync
        def _(sp):
            def load_x(t):
                if t >= 2:
                    sp.wait_ge(s["xn1"], t - 1)
                sp.dma_start(x_in[:, t % 2, :], xf[t * P:(t + 1) * P, :]).then_inc(s[f"xl{t % 2}"], 16)

            def load_res(t):
                if t >= 2:
                    sp.wait_ge(s["x2_s"], t - 1)
                sp.dma_start(x_res[:, t % 2, :], xf[t * P:(t + 1) * P, :]).then_inc(s[f"xr{t % 2}"], 16)

            def store_tile(t):
                sp.wait_ge(s["x2_s"], t + 1)
                sp.dma_start(out[t * P:(t + 1) * P, :], x2[:, :]).then_inc(s["x2_out"], 16)
                sp.wait_ge(s["xn2_s"], t + 1)
                sp.dma_start(xn2_d[t * P:(t + 1) * P, :], xn2[:, :]).then_inc(s["xn2_out"], 16)

            load_x(0)
            load_x(1)
            for k in chunks:
                if k:
                    sp.wait_ge(s["w_lo"], k)
                sp.dma_start(w_raw[:, :], w_qkv[k * P:(k + 1) * P, :]).then_inc(s["w_in"], 16)
                if k < 2:
                    load_x(2 + k)
            for c in chunks:
                if c == 0:
                    sp.wait_ge(s["w_lo"], KC)
                sp.dma_start(w_raw[:, 0:D], w_out[c * P:(c + 1) * P, :]).then_inc(s["w_out_in"], 16)
                sp.wait_ge(s["w_lo"], KC + c + 1)
            sp.dma_start(gw[:, :, :], gate_w.rearrange("(k p) e -> p k e", p=P)).then_inc(s["gw_in"], 16)
            load_res(0)
            load_res(1)
            for n in range(NB + 1):
                if n + 1 < NB:
                    for t in range(TPB):
                        load_x((n + 1) * TPB + t)
                if n:
                    for t in range((n - 1) * TPB, n * TPB):
                        store_tile(t)
                        if t + 2 < NT:
                            load_res(t + 2)
            sp.wait_ge(s["gate_mm"], NT)
            sp.wait_ge(s["x2_out"], 16 * NT)
            sp.wait_ge(s["xn2_out"], 16 * NT)
            shared = [(sg[:, :, :], sw_gate.rearrange("(k p) f -> p k f", p=P)),
                      (su[:, :, :], sw_up.rearrange("(k p) f -> p k f", p=P))]
            for h in range(HALVES):
                r0 = h * F
                full = (FC - 1) * P
                shared += [(sd[:, h, 0:FC - 1, :], sw_down[r0:r0 + full, :].rearrange("(c p) d -> p c d", p=P)),
                           (sd[0:FROWS[-1], h, FC - 1, :], sw_down[r0 + full:r0 + F, :])]

            def load_job_x(t):
                if t >= 2:
                    sp.wait_ge(s["turned_x"], t - 1)
                sp.dma_start(x_job[:, t % 2, :], xn2_d[t * P:(t + 1) * P, :]).then_inc(s[f"xin{t % 2}"], 16)

            load_job_x(0)
            load_job_x(1)
            for dst, src in shared:
                sp.dma_start(dst, src).then_inc(s["shared_in"], 16)
            for e in range(E):
                full = (FC - 1) * P
                sp.dma_start(wg[:, e], w_gate[e].rearrange("(k p) f -> p k f", p=P)).then_inc(s["routed_in"], 16)
                sp.dma_start(wu[:, e], w_up[e].rearrange("(k p) f -> p k f", p=P)).then_inc(s["routed_in"], 16)
                sp.dma_start(wd[:, e, 0:FC - 1, :], w_down[e, 0:full, :].rearrange("(c p) d -> p c d", p=P))\
                  .then_inc(s["routed_in"], 16)
                sp.dma_start(wd[0:FROWS[-1], e, FC - 1, :], w_down[e, full:F, :]).then_inc(s["routed_in"], 16)
            for t in range(2, NT):
                load_job_x(t)
            for q in range(2):
                sp.wait_ge(s[f"yo{q}"], 16 * ((NT + JOBS - 1 - q) // 2 + 1))

        SHARED_DMAS = 2 + 2 * HALVES
        ROUTED_DMAS = 4 * E

        @block.gpsimd
        def _(pool):
            step = [0]

            def const(ins):
                step[0] += 1
                ins.then_inc(s["cst_a"], 1)
                pool.wait_ge(s["cst_a"], step[0])

            def band(ap, pattern, base, mult):
                const(pool.affine_select(out=ap, in_=ap, compare_op=ALU.is_ge, fill=0.0, base=base,
                                         pattern=pattern, channel_multiplier=mult))

            for g in range(P // DH):
                pool.dma_start(dec[g * DH:(g + 1) * DH, :], bass.AP(decay.tensor, g, [[0, DH], [P // DH, KC]]),
                               allow_slow_non_contiguous=True).then_inc(s["dec_in"], 16)
            const(pool.memset(ident[:, :], 0.0))
            const(pool.affine_select(out=ident[:, :], in_=ident[:, :], compare_op=ALU.not_equal, fill=1.0,
                                     base=0, pattern=[[-1, P]], channel_multiplier=1))
            const(pool.memset(neg_half[:, :], -0.5))
            pool.nop().then_inc(s["consts"], 1)

            def rstd_of(mv, ve, rs, gate, value, got, done):
                pool.wait_ge(s[gate], value)
                pool.tensor_scalar(ve, mv, LN_EPS, None, ALU.add).then_inc(s[got], 1)
                pool.wait_ge(s[got], value)
                pool.tensor_tensor(rs, ve, neg_half[:, :], ALU.pow).then_inc(s[done], 1)

            def rstd_1(t):
                b = t % 2
                rstd_of(mean_var[:, b, 1:2], var_eps[:, b:b + 1], rstd[:, b:b + 1], "var1", t + 1, "veps1", "rstd1")

            def rstd_2(t):
                rstd_of(mean_var2[:, 1:2], var_eps2[:, :], rstd2[:, :], "var2", t + 1, "veps2", "rstd2_s")

            for t in range(TPB):
                rstd_1(t)
            for ap, pat in ((head_of, [[P, KC], [-DH, HEADS]]),):
                const(pool.memset(ap[:, :, :], 1.0))
                band(ap[:, :, :], pat, 0, 1)
                band(ap[:, :, :], [[-a, b] for a, b in pat], DH - 1, -1)
            const(pool.memset(of_head[:, :, :], 1.0))
            band(of_head[:, :, :], [[P, KC], [1, P]], 0, -DH)
            band(of_head[:, :, :], [[-P, KC], [-1, P]], DH - 1, DH)
            pool.nop().then_inc(s["consts"], 1)
            for n in range(NB + 1):
                if n + 1 < NB:
                    for t in range(TPB):
                        rstd_1((n + 1) * TPB + t)
                if n:
                    for t in range(TPB):
                        rstd_2((n - 1) * TPB + t)
            pool.wait_ge(s["gate_mm"], NT)
            pool.wait_ge(s["x2_out"], 16 * NT)
            pool.wait_ge(s["xn2_out"], 16 * NT)
            const(pool.memset(zeros[:, :], 0.0))
            for ap in (out, xn2_d):
                for a in range(8):
                    pool.dma_start(ap[T:ROWS, a * (D // 8):(a + 1) * (D // 8)], zeros[:, :])\
                        .then_inc(s["pad_out"], 16)
            const(pool.memset(ones[:, :], 1.0))
            const(pool.memset(tri[:, :], 1.0))
            band(tri[:, :], [[1, P]], -1, -1)
            const(pool.memset(not_first[:, :, :], 1.0))
            const(pool.memset(not_first[:, :, 0:1], 0.0))
            for ap, pat, b0, mult in ((iota_e, [[1, E]], 0, 0), (iota_j, [[1, JW]], 0, 0),
                                      (iota_p, [[1, P]], 0, 0), (token_1, [[P, NT]], 1, 1),
                                      (spare, [[0, 1]], T + 1, 1)):
                const(pool.iota(ap[:, :], pattern=pat, base=b0, channel_multiplier=mult,
                                allow_small_or_imprecise_dtypes=True))
            pool.nop().then_inc(s["cst_b"], 1)

            def prev_out(t):
                return s[f"yo{(t - 1) % 2}"], 16 * ((t - 1) // 2 + 1)

            def add_shared(t):
                pool.wait_ge(s["y_s"], t + 1)
                pool.dma_start(out[t * P:(t + 1) * P, :], y_job[:, t % 2, :], accum_op=ALU.add)\
                    .then_inc(s[f"yo{t % 2}"], 16)

            def gather(r, b):
                pool.tensor_copy(idx_in[:, b:b + 1], job_tok[:, bass.ds(r, 1)]).then_inc(s["idxg_s"], 1)
                seen, free = pool.to_reg(r + 1), pool.to_reg(NT + r - 1)
                pool.wait_ge(s["xn2_out"], 16 * NT)
                pool.wait_ge(s["idxg_s"], seen)
                pool.wait_ge(s["turned_x"], free)
                pool.indirect_dma_start(x_job[:, b, :], None, xn2_d[:, :],
                                        bass.IndirectOffsetOnAxis(idx_in[:, b:b + 1], 0))\
                    .then_inc(s[f"gin{b}"], 16)

            def scatter(r, b):
                pool.wait_ge(s[f"yo{1 - b}"], 16 * (NT // 2) + 8 * (r + b))
                pool.tensor_copy(idx_out[:, b:b + 1], job_tok[:, bass.ds(r, 1)]).then_inc(s["idxs_s"], 1)
                seen, ready = pool.to_reg(r + 1), pool.to_reg(NT + r + 1)
                pool.wait_ge(s["x2_out"], 16 * NT)
                pool.wait_ge(s["idxs_s"], seen)
                pool.wait_ge(s["y_s"], ready)
                pool.indirect_dma_start(out[:, :], bass.IndirectOffsetOnAxis(idx_out[:, b:b + 1], 0),
                                        y_job[:, b, :], None, compute_op=ALU.add).then_inc(s[f"yo{b}"], 16)

            for t in range(NT - 2):
                add_shared(t)
            pool.wait_ge(s["tables_s"], 1)
            pool.wait_ge(s["pad_out"], 16 * 16)
            gather(0, 0)
            gather(1, 1)
            add_shared(NT - 2)
            add_shared(NT - 1)
            with pool.Fori(0, JOBS // 2 - 1) as i:
                for b in range(2):
                    scatter(2 * i + b, b)
                    gather(2 * i + b + 2, b)
            r = 2 * (JOBS // 2 - 1)
            scatter(r, 0)
            gather(r + 2, 0)
            scatter(r + 1, 1)
            scatter(r + 2, 0)

        @block.scalar
        def _(act):
            act.wait_ge(s["dec_in"], 16 * (P // DH))
            act.activation(dec[:, :], dec[:, :], ACT.Exp, scale=-1.0).then_inc(s["dec_e"], 1)

            def hi_x(t):
                act.wait_ge(s["turned1"], t + 1)
                if t >= 2 * TPB:
                    act.wait_ge(s["q_mm"], KC * (t // TPB - 1))
                n, j = t // TPB, t % TPB
                act.copy(xnT_h[:, n % 2, :, j * P:(j + 1) * P], turn[:, :, :]).then_inc(s["hi1"], 1)

            def hi_w(k):
                if k < KC:
                    act.wait_ge(s["w_in"], 16 * (k + 1))
                    act.copy(wq_h[:, k, :], w_raw[:, :]).then_inc(s["w_hi"], 1)
                else:
                    act.wait_ge(s["w_out_in"], 16 * (k - KC + 1))
                    act.copy(wo_h[:, k - KC, :], w_raw[:, 0:D]).then_inc(s["w_hi"], 1)

            def phi_parts(n, c, which):
                i = n * KC + c
                item = k_item if which == 0 else q_item
                act.wait_ge(s["k_mm" if which == 0 else "q_mm"], i + 1)
                if i:
                    act.wait_ge(s["phik_s" if which == 0 else "phiq_s"], i)
                z = ring[item(n, c) % RING]
                act.activation(exp_z[:, which, :], z[:, :], ACT.Exp)
                act.activation(relu_z[:, which, :], z[:, :], ACT.Relu)\
                    .then_inc(s["k_act" if which == 0 else "q_act"], 1)

            def hi_a(n, c):
                i = n * KC + c
                act.wait_ge(s["a_s"], i + 1)
                if n:
                    act.wait_ge(s["out_mm"], n * TPB)
                act.copy(at_h[:, c, :], num[:, n % 2, c, :]).then_inc(s["ah_s"], 1)

            def move_xn2T(t):
                act.wait_ge(s["turned2"], t + 1)
                if t:
                    act.wait_ge(s["gate_mm"], t)
                act.copy(xn2T[:, :, :], turn[:, :, :]).then_inc(s["xn2T_s"], 1)

            hi_w(0)
            hi_x(0)
            hi_w(1)
            hi_x(1)
            hi_w(2)
            hi_x(2)
            hi_w(3)
            hi_x(3)
            for c in chunks:
                hi_w(KC + c)
            for n in blocks:
                for c in chunks:
                    phi_parts(n, c, 0)
                    phi_parts(n, c, 1)
                    if n and c == 1:
                        for a in chunks:
                            hi_a(n - 1, a)
                    if n + 1 < NB and c in (1, 2):
                        for t in (0, 1):
                            hi_x((n + 1) * TPB + 2 * (c - 1) + t)
                    if n and c == 3:
                        for t in range(TPB):
                            move_xn2T((n - 1) * TPB + t)
            for a in chunks:
                hi_a(NB - 1, a)
            for t in range(TPB):
                move_xn2T((NB - 1) * TPB + t)

            def move_xT(t, b):
                act.wait_ge(s["turned_x"], t + 1)
                act.copy(xT[:, b], turn_x[:, :, :]).then_inc(s["xT_s"], 1)

            def gate_silu(u, b, first=False):
                act.wait_ge(s["gu_mm"], u + 1)
                if not first:
                    act.wait_ge(s["hid_s"], u - 1)
                act.activation(silu[:, b, :], ps_g[b][:, 0:F], ACT.Silu).then_inc(s["silu_s"], 1)

            def move_y(t, b, first=False):
                act.wait_ge(s["y_mm"], t + 1)
                if not first:
                    act.wait_ge(s[f"yo{b}"], 8 * (t - b))
                act.copy(y_job[:, b, :], ps_y[b][:, :]).then_inc(s["y_s"], 1)

            act.wait_ge(s["gate_mm"], NT)
            act.wait_ge(s["x2_out"], 16 * NT)
            act.wait_ge(s["xn2_out"], 16 * NT)
            move_xT(0, 0)
            act.wait_ge(s["rt_exp_in"], 1)
            act.activation(tab_a[:, :, :], tab_a[:, :, :], ACT.Exp).then_inc(s["rt_exp"], 1)

            def two_tiles(i, first=False):
                u, t = 4 * i, 2 * i
                gate_silu(u + 1, 1, first)
                move_xT(t + 1, 1)
                gate_silu(u + 2, 0)
                move_y(t, 0, first)
                gate_silu(u + 3, 1)
                move_xT(t + 2, 0)
                gate_silu(u + 4, 0)
                move_y(t + 1, 1, first)

            gate_silu(0, 0, True)
            two_tiles(0, first=True)
            with act.Fori(1, NT // 2) as i:
                two_tiles(i)
            with act.Fori(0, JOBS // 2) as i:
                for b in (1, 2):
                    move_xT(NT + 2 * i + b, b % 2)
                    gate_silu(HALVES * NT + 2 * i + b, b % 2)

        @block.vector
        def _(dve):
            loc = [0]

            def link(ins):
                loc[0] += 1
                ins.then_inc(s["d_route"], 1)
                dve.wait_ge(s["d_route"], loc[0])

            dve.wait_ge(s["dec_e"], 1)
            dve.tensor_scalar(dec[:, :], dec[:, :], 1.0, None, ALU.add).then_inc(s["dec_1"], 1)
            dve.wait_ge(s["dec_1"], 1)
            dve.reciprocal(dec[:, :], dec[:, :]).then_inc(s["dec_ok"], 1)

            def stats_x(t):
                b = t % 2
                dve.wait_ge(*tile_sem("xl", t))
                if t >= 2:
                    dve.wait_ge(s["xn1"], t - 1)
                dve.bn_stats(stats[:, b, :], x_in[:, b, :]).then_inc(s["stat1"], 1)
                dve.wait_ge(s["stat1"], t + 1)
                dve.bn_aggr(mean_var[:, b, :], stats[:, b, :]).then_inc(s["var1"], 1)

            def norm_x(t):
                b = t % 2
                dve.wait_ge(s["var1"], t + 1)
                dve.wait_ge(s["rstd1"], t + 1)
                if t:
                    dve.wait_ge(s["turned1"], t)
                dve.tensor_scalar(xn[:, :], x_in[:, b, :], mean_var[:, b, 0:1], rstd[:, b:b + 1],
                                  ALU.subtract, ALU.mult).then_inc(s["xn1"], 1)

            def lo_x(t):
                n, j = t // TPB, t % TPB
                at = (slice(None), n % 2, slice(None), slice(j * P, (j + 1) * P))
                dve.wait_ge(s["hi1"], t + 1)
                dve.tensor_tensor(xnT_l[at], turn[:, :, :], xnT_h[at].bitcast(F32), ALU.subtract)\
                    .then_inc(s["lo1"], 1)

            def lo_w(k):
                dve.wait_ge(s["w_hi"], k + 1)
                if k < KC:
                    dve.tensor_tensor(wq_l[:, k, :], w_raw[:, :], wq_h[:, k, :].bitcast(F32), ALU.subtract)\
                        .then_inc(s["w_lo"], 1)
                else:
                    dve.tensor_tensor(wo_l[:, k - KC, :], w_raw[:, 0:D], wo_h[:, k - KC, :].bitcast(F32),
                                      ALU.subtract).then_inc(s["w_lo"], 1)

            def chunk(n, c):
                i = n * KC + c
                dcol = dec[:, c:c + 1].broadcast_to([P, BLK])
                dve.wait_ge(s["k_act"], i + 1)
                if i:
                    for name in ("kv_s", "sk_s", "skv_s", "qk_s", "num_s"):
                        dve.wait_ge(s[name], i)
                    dve.wait_ge(s["carry_s"], 2 * i)
                dve.scalar_tensor_tensor(out=phi_k[:, :], in0=exp_z[:, 0, :], scalar=1.0, in1=relu_z[:, 0, :],
                                         op0=ALU.min, op1=ALU.add).then_inc(s["phik_s"], 1)
                dve.wait_ge(s["phik_s"], i + 1)
                dve.wait_ge(s["v_mm"], i + 1)
                dve.tensor_tensor(kv[:, :], phi_k[:, :], ring[v_item(n, c) % RING][:, :], ALU.mult)\
                    .then_inc(s["kv_s"], 1)
                start = n % BPS == 0
                if not start:
                    dve.wait_ge(s["carry_s"], 2 * (i - KC + 1))
                dve.tensor_tensor_scan(run_k[:, :], dcol, phi_k[:, :], 0.0 if start else carry[:, 0, c:c + 1],
                                       ALU.mult, ALU.add).then_inc(s["sk_s"], 1)
                dve.wait_ge(s["kv_s"], i + 1)
                dve.tensor_tensor_scan(run_kv[:, :], dcol, kv[:, :], 0.0 if start else carry[:, 1, c:c + 1],
                                       ALU.mult, ALU.add).then_inc(s["skv_s"], 1)
                dve.wait_ge(s["q_act"], i + 1)
                dve.scalar_tensor_tensor(out=phi_q[:, :], in0=exp_z[:, 1, :], scalar=1.0, in1=relu_z[:, 1, :],
                                         op0=ALU.min, op1=ALU.add).then_inc(s["phiq_s"], 1)
                dve.wait_ge(s["sk_s"], i + 1)
                dve.tensor_copy(carry[:, 0, c:c + 1], run_k[:, BLK - 1:BLK]).then_inc(s["carry_s"], 1)
                dve.wait_ge(s["phiq_s"], i + 1)
                if i >= 2:
                    dve.wait_ge(s["den_mm"], i - 1)
                dve.tensor_tensor(qk[:, c % 2, :], phi_q[:, :], run_k[:, :], ALU.mult).then_inc(s["qk_s"], 1)
                dve.wait_ge(s["skv_s"], i + 1)
                dve.tensor_copy(carry[:, 1, c:c + 1], run_kv[:, BLK - 1:BLK]).then_inc(s["carry_s"], 1)
                if n >= 2:
                    dve.wait_ge(s["al_s"], (n - 2) * KC + c + 1)
                    dve.wait_ge(s["ah_s"], (n - 2) * KC + c + 1)
                dve.tensor_tensor(num[:, n % 2, c, :], phi_q[:, :], run_kv[:, :], ALU.mult).then_inc(s["num_s"], 1)

            def denominators(n):
                dve.wait_ge(s["den_mm"], (n + 1) * KC)
                if n:
                    dve.wait_ge(s["rden_s"], n)
                dve.tensor_scalar(den[:, :], ps_den[0:HEADS, :], DEN_EPS, None, ALU.max).then_inc(s["den_max"], 1)
                dve.wait_ge(s["den_max"], n + 1)
                if n:
                    dve.wait_ge(s["ex_mm"], n * KC)
                dve.reciprocal(rden[:, :], den[:, :]).then_inc(s["rden_s"], 1)

            def divide(n):
                for c in chunks:
                    i = n * KC + c
                    dve.wait_ge(s["ex_mm"], i + 1)
                    dve.wait_ge(s["num_s"], i + 1)
                    a = num[:, n % 2, c, :]
                    dve.tensor_tensor(a, a, ring[items[(n, c, "ex")] % RING][:, :], ALU.mult).then_inc(s["a_s"], 1)
                for c in chunks:
                    i = n * KC + c
                    dve.wait_ge(s["ah_s"], i + 1)
                    dve.tensor_tensor(at_l[:, c, :], num[:, n % 2, c, :], at_h[:, c, :].bitcast(F32), ALU.subtract)\
                        .then_inc(s["al_s"], 1)

            def norm_2(t):
                dve.wait_ge(s["out_mm"], t + 1)
                dve.wait_ge(*tile_sem("xr", t))
                if t:
                    dve.wait_ge(s["x2_out"], 16 * t)
                    dve.wait_ge(s["xn2_s"], t)
                n, j = t // TPB, t % TPB
                dve.tensor_tensor(x2[:, :], ring[items[(n, j, "out")] % RING][:, :], x_res[:, t % 2, :], ALU.add)\
                    .then_inc(s["x2_s"], 1)
                dve.wait_ge(s["x2_s"], t + 1)
                dve.bn_stats(stats2[:, :], x2[:, :]).then_inc(s["stat2"], 1)
                dve.wait_ge(s["stat2"], t + 1)
                dve.bn_aggr(mean_var2[:, :], stats2[:, :]).then_inc(s["var2"], 1)
                dve.wait_ge(s["var2"], t + 1)
                dve.wait_ge(s["rstd2_s"], t + 1)
                if t:
                    dve.wait_ge(s["xn2_out"], 16 * t)
                    dve.wait_ge(s["turned2"], t)
                dve.tensor_scalar(xn2[:, :], x2[:, :], mean_var2[:, 0:1], rstd2[:, :], ALU.subtract, ALU.mult)\
                    .then_inc(s["xn2_s"], 1)

            stats_x(0)
            stats_x(1)
            norm_x(0)
            lo_w(0)
            lo_x(0)
            norm_x(1)
            stats_x(2)
            lo_w(1)
            lo_x(1)
            norm_x(2)
            stats_x(3)
            lo_w(2)
            lo_x(2)
            norm_x(3)
            lo_w(3)
            lo_x(3)
            for c in chunks:
                lo_w(KC + c)
            for n in blocks:
                for c in chunks:
                    chunk(n, c)
                    more = n + 1 < NB
                    t = (n + 1) * TPB
                    if n and c == 0:
                        denominators(n - 1)
                    if more and c == 0:
                        stats_x(t)
                        stats_x(t + 1)
                    if n and c == 1:
                        divide(n - 1)
                    if more and c == 1:
                        norm_x(t)
                        stats_x(t + 2)
                        lo_x(t)
                        norm_x(t + 1)
                        stats_x(t + 3)
                        lo_x(t + 1)
                    if more and c == 2:
                        norm_x(t + 2)
                        lo_x(t + 2)
                        norm_x(t + 3)
                        lo_x(t + 3)
                    if n and c == 2:
                        for j in range(TPB):
                            norm_2((n - 1) * TPB + j)
            denominators(NB - 1)
            divide(NB - 1)
            for j in range(TPB):
                norm_2((NB - 1) * TPB + j)
            dve.wait_ge(s["gate_mm"], NT)
            dve.tensor_copy(logits[:, :, :], ps_gate[:, :, 0:E]).then_inc(s["logit_s"], 1)
            dve.wait_ge(s["x2_out"], 16 * NT)
            dve.wait_ge(s["xn2_out"], 16 * NT)
            dve.wait_ge(s["logit_s"], 1)

            wide = lambda ap: ap.unsqueeze(2).broadcast_to([P, NT, E])
            link(dve.tensor_reduce(row_a[:, :], logits[:, :, :], AX_X, ALU.max))
            dve.tensor_tensor(tab_a[:, :, :], logits[:, :, :], wide(row_a[:, :]), ALU.subtract)\
                .then_inc(s["rt_exp_in"], 1)
            dve.wait_ge(s["rt_exp"], 1)
            link(dve.tensor_reduce(row_a[:, :], tab_a[:, :, :], AX_X, ALU.add))
            link(dve.reciprocal(row_b[:, :], row_a[:, :]))
            link(dve.tensor_tensor(score[:, :, :], tab_a[:, :, :], wide(row_b[:, :]), ALU.mult))
            for t in range(NT):
                ins = dve.max(top[:, t, :], score[:, t, :])
            link(ins)
            for t in range(NT):
                ins = dve.max_index(top_i[:, t, :], top[:, t, :], score[:, t, :])
            link(ins)
            dve.wait_ge(s["cst_b"], 1)
            link(dve.tensor_copy(top_f[:, :, :], top_i[:, :, 0:TOPK].rearrange("p t k -> p k t")))
            over_t = iota_e[:, :].unsqueeze(1).broadcast_to([P, NT, E])
            for k in range(TOPK):
                ins = dve.tensor_tensor(pick[:, k], wide(top_f[:, k, :]), over_t, ALU.is_equal)
            link(ins)
            dve.tensor_tensor(picked[:, :, :], pick[:, 0], pick[:, 1], ALU.add).then_inc(s["picked_s"], 1)
            dve.wait_ge(s["rank_mm"], 1)
            ranks = ps_rank[:, 0:P].rearrange("p (t e) -> p t e", e=E)
            totals = ps_rank[:, P:2 * P].rearrange("p (t e) -> p e t", e=E)
            link(dve.tensor_copy(count[:, :, :], totals))
            flat = lambda ap: ap.rearrange("p e t -> p (e t)")
            link(dve.tensor_tensor_scan(flat(upto[:, :, :]), flat(not_first[:, :, :]), flat(count[:, :, :]), 0.0,
                                        ALU.mult, ALU.add))
            link(dve.tensor_scalar(jobs_i[:, :], upto[:, :, NT - 1], float(P - 1), None, ALU.add))
            link(dve.tensor_scalar(jobs_i[:, :], jobs_i[:, :], 7, None, ALU.arith_shift_right))
            link(dve.tensor_copy(jobs_f[:, :], jobs_i[:, :]))
            link(dve.tensor_tensor_scan(jobs_end[:, :], ones[:, 0:E], jobs_f[:, :], 0.0, ALU.mult, ALU.add))
            link(dve.tensor_tensor(jobs_beg[:, :], jobs_end[:, :], jobs_f[:, :], ALU.subtract))
            link(dve.tensor_tensor(base[:, :, :], upto[:, :, :], count[:, :, :], ALU.subtract))
            link(dve.tensor_scalar(jobs_beg[:, :], jobs_beg[:, :], float(P), None, ALU.mult))
            link(dve.tensor_tensor(base[:, :, :], base[:, :, :],
                                   jobs_beg[:, :].unsqueeze(2).broadcast_to([P, E, NT]), ALU.add))
            link(dve.tensor_tensor(slot_e[:, :, :], ranks, base[:, :, :].rearrange("p e t -> p t e"), ALU.add))
            for k in range(TOPK):
                link(dve.tensor_tensor(tab_a[:, :, :], slot_e[:, :, :], pick[:, k], ALU.mult))
                link(dve.tensor_reduce(slot_f[:, k, :], tab_a[:, :, :], AX_X, ALU.add))
            link(dve.tensor_copy(slot_i[:, :], slot_f[:, :, :].rearrange("p k t -> p (k t)")))
            link(dve.tensor_scalar(slot_ji[:, :], slot_i[:, :], 7, None, ALU.arith_shift_right))
            link(dve.tensor_scalar(slot_pi[:, :], slot_i[:, :], P - 1, None, ALU.bitwise_and))
            link(dve.tensor_copy(slot_j[:, :], slot_ji[:, :]))
            link(dve.tensor_copy(slot_p[:, :], slot_pi[:, :]))
            link(dve.tensor_tensor(past[:, :, :], iota_j[:, :].unsqueeze(2).broadcast_to([P, JW, E]),
                                   jobs_end[:, :].unsqueeze(1).broadcast_to([P, JW, E]), ALU.is_ge))
            link(dve.tensor_reduce(job_ef[:, :], past[:, :, :], AX_X, ALU.add))
            link(dve.tensor_scalar(job_e[:, :], job_ef[:, :], float(E - 1), None, ALU.min))
            for m in range(TOPK * NT):
                k, t = m // NT, m % NT
                if m >= 2:
                    dve.wait_ge(s["acc_mm"], m - 1)
                dve.tensor_scalar(hot_p[:, m % 2, :], iota_p[:, :], slot_p[:, m:m + 1], None, ALU.is_equal)
                dve.tensor_scalar(hot_j[:, m % 2, 0, :], iota_j[:, :], slot_j[:, m:m + 1], token_1[:, t:t + 1],
                                  ALU.is_equal, ALU.mult)
                dve.tensor_scalar(hot_j[:, m % 2, 1, :], iota_j[:, :], slot_j[:, m:m + 1], top[:, t, k:k + 1],
                                  ALU.is_equal, ALU.mult).then_inc(s["hot_s"], 1)
            dve.wait_ge(s["acc_mm"], TOPK * NT)
            link(dve.tensor_copy(job_tok1[:, :], ps_acc[:, 0:JW]))
            link(dve.tensor_copy(job_w[:, :], ps_acc[:, JW:2 * JW]))
            link(dve.tensor_scalar(job_pad[:, :], job_tok1[:, :], 0.0, spare[:, 0:1], ALU.is_equal, ALU.mult))
            dve.scalar_tensor_tensor(out=job_tok[:, :], in0=job_tok1[:, :], scalar=-1.0, in1=job_pad[:, :],
                                     op0=ALU.add, op1=ALU.add).then_inc(s["tables_s"], 1)
            dve.wait_ge(s["tables_s"], 1)

            def hidden(u, b, first=False):
                dve.wait_ge(s["silu_s"], u + 1)
                if not first:
                    dve.wait_ge(s["turned_h"], u - 1)
                dve.tensor_tensor(hid[:, b, :], ps_u[b][:, 0:F], silu[:, b, :], ALU.mult).then_inc(s["hid_s"], 1)

            def move_hidT(u, b):
                dve.wait_ge(s["turned_h"], u + 1)
                for c, rows in enumerate(FROWS):
                    pass
                dve.tensor_copy(hidT[:, b, 0:FC - 1, :], turn_h[:, 0:FC - 1, :])
                dve.tensor_copy(hidT[0:FROWS[-1], b, FC - 1, :], turn_h[0:FROWS[-1], FC - 1, :])\
                    .then_inc(s["hidT_s"], 1)

            def weigh_y(r, b):
                t = NT + r
                dve.wait_ge(s["y_mm"], t + 1)
                dve.wait_ge(s[f"yo{b}"], 8 * (t - b))
                dve.tensor_scalar(y_job[:, b, :], ps_y[b][:, :], job_w[:, bass.ds(r, 1)], None, ALU.mult)\
                    .then_inc(s["y_s"], 1)

            def four(u, first=False):
                hidden(u + 1, 1, first)
                move_hidT(u, 0)
                hidden(u + 2, 0)
                move_hidT(u + 1, 1)
                hidden(u + 3, 1)
                move_hidT(u + 2, 0)

            hidden(0, 0, True)
            four(0, True)
            with dve.Fori(1, NT // 2) as i:
                hidden(4 * i, 0)
                move_hidT(4 * i - 1, 1)
                four(4 * i)
            R0 = HALVES * NT
            hidden(R0, 0)
            move_hidT(R0 - 1, 1)
            with dve.Fori(0, JOBS // 2) as i:
                hidden(R0 + 2 * i + 1, 1)
                move_hidT(R0 + 2 * i, 0)
                weigh_y(2 * i, 0)
                hidden(R0 + 2 * i + 2, 0)
                move_hidT(R0 + 2 * i + 1, 1)
                weigh_y(2 * i + 1, 1)
            move_hidT(R0 + JOBS - 1, 0)
            weigh_y(JOBS - 1, 0)

_INS = ['L0_attn_x', 'L0_attn_w_qkv', 'L0_attn_w_out', 'L0_attn_decay_param', 'L0_ffn_gate_w', 'L0_ffn_w_gate',
        'L0_ffn_w_up', 'L0_ffn_w_down', 'L0_ffn_sw_gate', 'L0_ffn_sw_up', 'L0_ffn_sw_down']


def kernel(**inputs):
    import numpy as _np
    import concourse.bacc as _bacc
    from concourse import mybir as _mybir
    from concourse.bass_utils import run_bass_kernel_spmd as _run

    nc = _bacc.Bacc("TRN2", target_bir_lowering=False, num_devices=1)
    arrays, args = {}, []
    for name in _INS:
        a = _np.ascontiguousarray(inputs[name])
        arrays[f"in_{name}_dram"] = a
        args.append(nc.dram_tensor(f"in_{name}_dram", a.shape, _mybir.dt.from_np(a.dtype), kind="ExternalInput").ap())
    B, S, D = inputs['L0_attn_x'].shape
    args.append(nc.dram_tensor("out_dram", (B * S + 128, D), _mybir.dt.float32, kind="ExternalOutput").ap())
    preln_decay_attention_moe(nc, *args)
    r = _run(nc, [arrays], core_ids=[0])
    return r.results[0]["out_dram"][:B * S].reshape(B, S, D)
```

```python
from contextlib import ExitStack

import concourse.bass as bass
from concourse import mybir

P = 128
F32 = mybir.dt.float32
F32R = mybir.dt.float32r
I32 = mybir.dt.int32
U32 = mybir.dt.uint32
ALU = mybir.AluOpType
ACT = mybir.ActivationFunctionType
AX_X = mybir.AxisListType.X

LN_EPS = 1e-5
DEN_EPS = 1e-6


def preln_decay_attention_moe(nc, x, w_qkv, w_out, decay, gate_w, w_gate, w_up, w_down,
                              sw_gate, sw_up, sw_down, out):
    B, S, D = x.shape
    T = B * S
    HEADS = decay.shape[0]
    DH = D // HEADS
    E, _, F = w_gate.shape
    KC = D // P
    NT = T // P
    BLK = 512
    TPB = BLK // P
    NB = T // BLK
    BPS = S // BLK
    HALVES = sw_gate.shape[1] // F
    assert HALVES == 2 and NT % 4 == 0 and D == BLK
    FROWS = [min(P, F - P * c) for c in range((F + P - 1) // P)]
    FC = len(FROWS)
    TOPK = 2
    JOBS = (TOPK * T - E) // P + E
    JOBS -= 1 if (TOPK * T + E * (P - 1)) // P < JOBS else 0
    JW = JOBS + JOBS % 2
    ROWS = T + P

    xf = x.rearrange("b s d -> (b s) d")
    xn2_d = nc.dram_tensor("xn2_scratch", [ROWS, D], F32, kind="Internal").ap()

    with ExitStack() as ctx:
        def sb(name, shape, dt=F32, stack=ctx):
            return stack.enter_context(nc.sbuf_tensor(name, shape, dt))

        def psum(name, shape, dt=F32, stack=ctx):
            return stack.enter_context(nc.psum_tensor(name, shape, dt))

        def sem(name):
            return ctx.enter_context(nc.semaphore(name))

        ident = sb("ident", [P, P])
        gw = sb("gw", [P, KC, E])
        logits = sb("logits", [P, NT, E])
        attn = ExitStack()
        asb = lambda name, shape, dt=F32: sb(name, shape, dt, attn)
        wq_h = asb("wq_h", [P, KC, 3 * D], F32R)
        wq_l = asb("wq_l", [P, KC, 3 * D], F32R)
        wo_h = asb("wo_h", [P, KC, D], F32R)
        wo_l = asb("wo_l", [P, KC, D], F32R)
        w_raw = asb("w_raw", [P, 3 * D])
        head_of = asb("head_of", [P, KC, HEADS])
        of_head = asb("of_head", [HEADS, KC, P])
        dec = asb("dec", [P, KC])
        carry = asb("carry", [P, 2, KC])
        x_in = asb("x_in", [P, 2, D])
        x_res = asb("x_res", [P, 2, D])
        stats = asb("stats", [P, 2, 6])
        mean_var = asb("mean_var", [P, 2, 2])
        var_eps = asb("var_eps", [P, 2])
        rstd = asb("rstd", [P, 2])
        stats2 = asb("stats2", [P, 2, 6])
        mean_var2 = asb("mean_var2", [P, 2, 2])
        var_eps2 = asb("var_eps2", [P, 2])
        rstd2 = asb("rstd2", [P, 2])
        neg_half = asb("neg_half", [P, 1])
        xn = asb("xn", [P, D])
        xnT_h = asb("xnT_h", [P, 2, KC, BLK], F32R)
        xnT_l = asb("xnT_l", [P, 2, KC, BLK], F32R)
        exp_z = asb("exp_z", [P, 2, BLK])
        relu_z = asb("relu_z", [P, 2, BLK])
        phi_k = asb("phi_k", [P, BLK])
        phi_q = asb("phi_q", [P, BLK])
        kv = asb("kv", [P, BLK])
        run_k = asb("run_k", [P, BLK])
        run_kv = asb("run_kv", [P, BLK])
        qk = asb("qk", [P, 2, BLK])
        num = asb("num", [P, 2, KC, BLK])
        den = asb("den", [HEADS, BLK])
        rden = asb("rden", [HEADS, BLK])
        at_h = asb("at_h", [P, KC, BLK], F32R)
        at_l = asb("at_l", [P, KC, BLK], F32R)
        x2 = asb("x2", [P, 2, D])
        xn2 = asb("xn2", [P, 2, D])
        xn2T = asb("xn2T", [P, KC, P])
        attn.close()
        moe = ExitStack()
        msb = lambda name, shape, dt=F32: sb(name, shape, dt, moe)
        wg = msb("wg", [P, E, KC, F])
        wu = msb("wu", [P, E, KC, F])
        wd = msb("wd", [P, E, FC, D])
        x_job = msb("x_job", [P, 2, D])
        xT = msb("xT", [P, 2, KC, P])
        silu = msb("silu", [P, 2, F])
        hid = msb("hid", [P, 2, F])
        hidT = msb("hidT", [P, 2, FC, P])
        y_job = msb("y_job", [P, 2, D])
        sg = msb("sg", [P, KC, HALVES * F])
        su = msb("su", [P, KC, HALVES * F])
        sd = msb("sd", [P, HALVES, FC, D])
        tri = msb("tri", [P, P])
        ones = msb("ones", [P, P])
        zeros = msb("zeros", [P, D // 8])
        iota_e = msb("iota_e", [P, E])
        iota_j = msb("iota_j", [P, JW])
        iota_p = msb("iota_p", [P, P])
        token_1 = msb("token_1", [P, NT])
        spare = msb("spare", [P, 1])
        not_first = msb("not_first", [P, E, NT])
        row_a = msb("row_a", [P, NT])
        row_b = msb("row_b", [P, NT])
        tab_a = msb("tab_a", [P, NT, E])
        score = msb("score", [P, NT, E])
        top = msb("top", [P, NT, 8])
        top_i = msb("top_i", [P, NT, 8], U32)
        top_f = msb("top_f", [P, TOPK, NT])
        pick = msb("pick", [P, TOPK, NT, E])
        picked = msb("picked", [P, NT, E])
        count = msb("count", [P, E, NT])
        upto = msb("upto", [P, E, NT])
        base = msb("base", [P, E, NT])
        slot_e = msb("slot_e", [P, NT, E])
        jobs_f = msb("jobs_f", [P, E])
        jobs_i = msb("jobs_i", [P, E], I32)
        jobs_end = msb("jobs_end", [P, E])
        jobs_beg = msb("jobs_beg", [P, E])
        slot_f = msb("slot_f", [P, TOPK, NT])
        slot_i = msb("slot_i", [P, TOPK * NT], I32)
        slot_ji = msb("slot_ji", [P, TOPK * NT], I32)
        slot_pi = msb("slot_pi", [P, TOPK * NT], I32)
        slot_j = msb("slot_j", [P, TOPK * NT])
        slot_p = msb("slot_p", [P, TOPK * NT])
        hot_p = msb("hot_p", [P, 2, P])
        hot_j = msb("hot_j", [P, 2, 2, JW])
        past = msb("past", [P, JW, E])
        job_ef = msb("job_ef", [P, JW])
        job_e = msb("job_e", [P, JW], I32)
        job_tok1 = msb("job_tok1", [P, JW])
        job_pad = msb("job_pad", [P, JW])
        job_tok = msb("job_tok", [P, JW], I32)
        job_w = msb("job_w", [P, JW])
        idx_in = msb("idx_in", [P, 2], I32)
        idx_out = msb("idx_out", [P, 2], I32)
        moe.close()

        pa = ExitStack()
        turn = psum("turn", [P, KC, P], stack=pa)
        RING = 5
        ring = [psum(f"ring{i}", [P, BLK], stack=pa) for i in range(RING)]
        ps_den = psum("ps_den", [P, BLK], stack=pa)
        ps_gate = psum("ps_gate", [P, NT, 4 * E], stack=pa)
        pa.close()
        pm = ExitStack()
        turn_x = psum("turn_x", [P, KC, P], stack=pm)
        turn_h = psum("turn_h", [P, 4, P], stack=pm)
        ps_g = [psum(f"ps_g{i}", [P, 512], stack=pm) for i in range(2)]
        ps_y = [psum(f"ps_y{i}", [P, D], stack=pm) for i in range(2)]
        ps_u = [psum(f"ps_u{i}", [P, 512], stack=pm) for i in range(2)]
        pm.close()

        names = """w_in w_out_in w_hi w_lo consts dec_in dec_e dec_1 dec_ok gw_in xl0 xl1 stat1 var1 veps1 rstd1
            xn1 turned1 hi1 lo1 k_mm v_mm q_mm k_act q_act phik_s kv_s sk_s skv_s carry_s phiq_s qk_s num_s
            den_mm den_max rden_s ex_mm a_s ah_s al_s out_mm xr0 xr1 x2_s stat2 var2 veps2 rstd2_s xn2_s
            turned2 xn2T_s gate_mm logit_s x2_out0 x2_out1 xn2_out0 xn2_out1 pad_out cst_a cst_b
            shared_in routed_in d_route rt_exp rt_exp_in rank_mm picked_s hot_s acc_mm tables_s
            xin0 xin1 gin0 gin1 turned_x xT_s gu_mm silu_s hid_s turned_h hidT_s y_mm y_s idxg_s idxs_s yo0 yo1""".split()
        s = {n: sem(n) for n in names}
        block = ctx.enter_context(nc.Block())

        blocks = range(NB)
        chunks = range(KC)
        ps_rank, ps_acc = ps_g[0], ps_g[1]
        SHARED_DMAS = 2 + 2 * HALVES
        ROUTED_DMAS = 4 * E
        items = {}
        k_item = lambda n, c: items[(n, c, "k")]
        q_item = lambda n, c: items[(n, c, "q")]
        v_item = lambda n, c: items[(n, c, "v")]
        release = []

        def bank(eng, freed_by, value):
            m = len(release)
            if m >= RING:
                eng.wait_ge(*release[m - RING])
            release.append((s[freed_by], value))
            return ring[m % RING]

        tile_sem = lambda pair, t: (s[f"{pair}{t % 2}"], 16 * (t // 2 + 1))

        def stores_done(eng):
            for name in ("x2_out0", "x2_out1", "xn2_out0", "xn2_out1"):
                eng.wait_ge(s[name], 8 * NT)

        @block.tensor
        def _(pe):
            def split_product(ps, pairs):
                steps = []
                for (ah, al), (bh, bl) in pairs:
                    steps += [(ah, bh), (ah, bl), (al, bh)]
                for i, (a, b) in enumerate(steps):
                    ins = pe.matmul(ps, a, b, start=(i == 0), stop=(i == len(steps) - 1))
                return ins

            turned = []

            def turn_free():
                if turned:
                    pe.wait_ge(*turned[-1])

            def turn_x1(t):
                pe.wait_ge(s["xn1"], t + 1)
                turn_free()
                turned.append((s["lo1"], t + 1))
                for k in chunks:
                    ins = pe.transpose(turn[:, k, :], xn[:, k * P:(k + 1) * P], ident[:, :])
                ins.then_inc(s["turned1"], 1)

            def project(n, c, z):
                i = n * KC + c
                name, freed = {0: ("q", "q_act"), 1: ("k", "k_act"), 2: ("v", "kv_s")}[z]
                items[(n, c, name)] = len(release)
                ps = bank(pe, freed, i + 1)
                pairs = []
                for k in chunks:
                    cols = slice(z * D + c * P, z * D + (c + 1) * P)
                    pairs.append(((wq_h[:, k, cols], wq_l[:, k, cols]), (xnT_h[:, n % 2, k, :], xnT_l[:, n % 2, k, :])))
                split_product(ps[:, :], pairs).then_inc(s[name + "_mm"], 1)

            def sum_heads(n, c):
                i = n * KC + c
                pe.wait_ge(s["qk_s"], i + 1)
                if n and c == 0:
                    pe.wait_ge(s["den_max"], n)
                pe.matmul(ps_den[0:HEADS, :], head_of[:, c, :], qk[:, c % 2, :], start=(c == 0), stop=(c == KC - 1))\
                    .then_inc(s["den_mm"], 1)

            def expand(n):
                pe.wait_ge(s["rden_s"], n + 1)
                for c in chunks:
                    items[(n, c, "ex")] = len(release)
                    ps = bank(pe, "a_s", n * KC + c + 1)
                    pe.matmul(ps[:, :], of_head[:, c, :], rden[:, :], start=True, stop=True).then_inc(s["ex_mm"], 1)

            def output(n, j):
                pe.wait_ge(s["al_s"], (n + 1) * KC)
                if n == 0 and j == 0:
                    pe.wait_ge(s["w_lo"], 2 * KC)
                items[(n, j, "out")] = len(release)
                ps = bank(pe, "x2_s", n * TPB + j + 1)
                tok = slice(j * P, (j + 1) * P)
                split_product(ps[:, :], [((at_h[:, k, tok], at_l[:, k, tok]), (wo_h[:, k, :], wo_l[:, k, :]))
                                         for k in chunks]).then_inc(s["out_mm"], 1)

            def turn_x2(t):
                pe.wait_ge(s["xn2_s"], t + 1)
                turn_free()
                turned.append((s["xn2T_s"], t + 1))
                for k in chunks:
                    ins = pe.transpose(turn[:, k, :], xn2[:, t % 2, k * P:(k + 1) * P], ident[:, :])
                ins.then_inc(s["turned2"], 1)

            def gate(t):
                if t == 0:
                    pe.wait_ge(s["gw_in"], 16)
                pe.wait_ge(s["xn2T_s"], t + 1)
                for k in chunks:
                    ins = pe.matmul(ps_gate[:, t, 0:E], xn2T[:, k, :], gw[:, k, :], start=(k == 0),
                                    stop=(k == KC - 1))
                ins.then_inc(s["gate_mm"], 1)

            pe.wait_ge(s["consts"], 1)
            for t in range(TPB):
                turn_x1(t)
            pe.wait_ge(s["w_lo"], KC)
            pe.wait_ge(s["consts"], 2)
            K, V, Q = 1, 2, 0
            for n in blocks:
                def before(step, *args):
                    if n:
                        step(n - 1, *args)

                def logit_steps(j):
                    if n >= 2:
                        if j:
                            gate((n - 2) * TPB + j - 1)
                        if j < TPB:
                            turn_x2((n - 2) * TPB + j)

                def next_x(j):
                    if n + 1 < NB:
                        turn_x1((n + 1) * TPB + j)

                pe.wait_ge(s["lo1"], (n + 1) * TPB)
                project(n, 0, K)
                before(sum_heads, KC - 1)
                project(n, 0, V)
                logit_steps(0)
                project(n, 0, Q)
                logit_steps(1)
                project(n, 1, K)
                sum_heads(n, 0)
                logit_steps(2)
                project(n, 1, V)
                logit_steps(3)
                before(expand)
                project(n, 1, Q)
                logit_steps(4)
                next_x(0)
                project(n, 2, K)
                sum_heads(n, 1)
                next_x(1)
                project(n, 2, V)
                next_x(2)
                project(n, 2, Q)
                next_x(3)
                before(output, 0)
                project(n, 3, K)
                sum_heads(n, 2)
                before(output, 1)
                project(n, 3, V)
                before(output, 2)
                project(n, 3, Q)
                before(output, 3)
            sum_heads(NB - 1, KC - 1)
            for j in range(TPB):
                if j:
                    gate((NB - 2) * TPB + j - 1)
                turn_x2((NB - 2) * TPB + j)
            gate((NB - 1) * TPB - 1)
            expand(NB - 1)
            for j in range(TPB):
                output(NB - 1, j)
            for t in range((NB - 1) * TPB, NT):
                turn_x2(t)
                gate(t)

            def turn_job(t, b, first=False, routed=None):
                if routed is None:
                    pe.wait_ge(s[f"xin{b}"], 8 * (t - b) + 16)
                else:
                    pe.wait_ge(s[f"gin{b}"], 8 * (routed - b) + 16)
                if not first:
                    pe.wait_ge(s["xT_s"], t)
                for k in chunks:
                    ins = pe.transpose(turn_x[:, k, :], x_job[:, b, k * P:(k + 1) * P], ident[:, :])
                ins.then_inc(s["turned_x"], 1)

            def gate_up(u, b, t, tb, w_g, w_u, first=False):
                pe.wait_ge(s["xT_s"], t + 1)
                if not first:
                    pe.wait_ge(s["hid_s"], u - 1)
                for ps, w in ((ps_g[b], w_g), (ps_u[b], w_u)):
                    for k in chunks:
                        ins = pe.matmul(ps[:, 0:F], xT[:, tb, k, :], w(k), start=(k == 0), stop=(k == KC - 1))
                ins.then_inc(s["gu_mm"], 1)

            def turn_hidden(u, b, first=False):
                pe.wait_ge(s["hid_s"], u + 1)
                if not first:
                    pe.wait_ge(s["hidT_s"], u)
                for c, rows in enumerate(FROWS):
                    ins = pe.transpose(turn_h[0:rows, c, :], hid[:, b, c * P:c * P + rows], ident[:, :])
                ins.then_inc(s["turned_h"], 1)

            def down(u, b, t, tb, w_d, start, stop, first=False):
                pe.wait_ge(s["hidT_s"], u + 1)
                if start and not first:
                    pe.wait_ge(s["y_s"], t - 1)
                for c, rows in enumerate(FROWS):
                    ins = pe.matmul(ps_y[tb][:, :], hidT[0:rows, b, c, :], w_d(c, rows),
                                    start=(start and c == 0), stop=(stop and c == FC - 1))
                if stop:
                    ins.then_inc(s["y_mm"], 1)

            def gate_up_shared(u, half, t, tb, first=False):
                cols = slice(half * F, (half + 1) * F)
                gate_up(u, half, t, tb, lambda k: sg[:, k, cols], lambda k: su[:, k, cols], first)

            def down_shared(u, half, t, tb, first=False, first_y=False):
                turn_hidden(u, half, first)
                down(u, half, t, tb, lambda c, rows: sd[0:rows, half, c, :], half == 0, half == 1, first_y)

            def gate_up_routed(r, b):
                e = pe.value_load(job_e[0:1, bass.ds(r, 1)], min_val=0, max_val=E - 1)
                gate_up(HALVES * NT + r, b, NT + r, b, lambda k: wg[:, e, k, :], lambda k: wu[:, e, k, :])
                return e

            def down_routed(r, b):
                e = pe.value_load(job_e[0:1, bass.ds(r, 1)], min_val=0, max_val=E - 1)
                u = HALVES * NT + r
                turn_hidden(u, b)
                down(u, b, NT + r, b, lambda c, rows: wd[0:rows, e, c, :], True, True)

            def rank_tokens():
                pe.wait_ge(s["picked_s"], 1)
                pe.matmul(ps_rank[:, 0:P], tri[:, :], picked[:, :, :].rearrange("p t e -> p (t e)"),
                          start=True, stop=True)
                pe.matmul(ps_rank[:, P:2 * P], ones[:, :], picked[:, :, :].rearrange("p t e -> p (t e)"),
                          start=True, stop=True).then_inc(s["rank_mm"], 1)

            def slot_tables():
                n = TOPK * NT
                for m in range(n):
                    pe.wait_ge(s["hot_s"], m + 1)
                    pe.matmul(ps_acc[:, 0:2 * JW], hot_p[:, m % 2, :], hot_j[:, m % 2].rearrange("p a j -> p (a j)"),
                              start=(m == 0), stop=(m == n - 1)).then_inc(s["acc_mm"], 1)

            pe.wait_ge(s["logit_s"], 1)
            turn_job(0, 0, True)
            pe.wait_ge(s["cst_b"], 1)
            rank_tokens()
            slot_tables()
            pe.wait_ge(s["shared_in"], 16 * SHARED_DMAS)
            pe.wait_ge(s["tables_s"], 1)
            gate_up_shared(0, 0, 0, 0, True)

            def two_tiles(i, first=False, last=False):
                u, t = 4 * i, 2 * i
                gate_up_shared(u + 1, 1, t, 0, first)
                down_shared(u, 0, t, 0, first, first)
                turn_job(t + 1, 1)
                gate_up_shared(u + 2, 0, t + 1, 1)
                down_shared(u + 1, 1, t, 0)
                gate_up_shared(u + 3, 1, t + 1, 1)
                down_shared(u + 2, 0, t + 1, 1, False, first)
                if not last:
                    turn_job(t + 2, 0)
                    gate_up_shared(u + 4, 0, t + 2, 0)
                    down_shared(u + 3, 1, t + 1, 1)

            two_tiles(0, first=True)
            with pe.Fori(1, NT // 2 - 1) as i:
                two_tiles(i)
            two_tiles(NT // 2 - 1, last=True)
            pe.wait_ge(s["routed_in"], 16 * ROUTED_DMAS)
            turn_job(NT, 0, routed=0)
            gate_up_routed(0, 0)
            down_shared(2 * NT - 1, 1, NT - 1, 1)
            with pe.Fori(0, JOBS // 2) as i:
                for b in range(2):
                    r = 2 * i + b
                    turn_job(NT + r + 1, 1 - b, routed=r + 1)
                    gate_up_routed(r + 1, 1 - b)
                    down_routed(r, b)
            down_routed(JOBS - 1, 0)

        @block.sync
        def _(sp):
            def load_x(t):
                if t >= 2:
                    sp.wait_ge(s["xn1"], t - 1)
                sp.dma_start(x_in[:, t % 2, :], xf[t * P:(t + 1) * P, :]).then_inc(s[f"xl{t % 2}"], 16)

            def load_res(t):
                if t >= 2:
                    sp.wait_ge(s["x2_s"], t - 1)
                sp.dma_start(x_res[:, t % 2, :], xf[t * P:(t + 1) * P, :]).then_inc(s[f"xr{t % 2}"], 16)

            def store_tile(t):
                sp.wait_ge(s["x2_s"], t + 1)
                sp.dma_start(out[t * P:(t + 1) * P, :], x2[:, t % 2, :]).then_inc(s[f"x2_out{t % 2}"], 16)
                sp.wait_ge(s["xn2_s"], t + 1)
                sp.dma_start(xn2_d[t * P:(t + 1) * P, :], xn2[:, t % 2, :]).then_inc(s[f"xn2_out{t % 2}"], 16)

            load_x(0)
            load_x(1)
            for k in chunks:
                if k:
                    sp.wait_ge(s["w_lo"], k)
                sp.dma_start(w_raw[:, :], w_qkv[k * P:(k + 1) * P, :]).then_inc(s["w_in"], 16)
                if k < 2:
                    load_x(2 + k)
            for c in chunks:
                if c == 0:
                    sp.wait_ge(s["w_lo"], KC)
                sp.dma_start(w_raw[:, 0:D], w_out[c * P:(c + 1) * P, :]).then_inc(s["w_out_in"], 16)
                sp.wait_ge(s["w_lo"], KC + c + 1)
            sp.dma_start(gw[:, :, :], gate_w.rearrange("(k p) e -> p k e", p=P)).then_inc(s["gw_in"], 16)
            load_res(0)
            load_res(1)
            for n in range(NB + 1):
                if n + 1 < NB:
                    for t in range(TPB):
                        load_x((n + 1) * TPB + t)
                if n:
                    for t in range((n - 1) * TPB, n * TPB):
                        store_tile(t)
                        if t + 2 < NT:
                            load_res(t + 2)
            sp.wait_ge(s["gate_mm"], NT)
            stores_done(sp)
            shared = [(sg[:, :, :], sw_gate.rearrange("(k p) f -> p k f", p=P)),
                      (su[:, :, :], sw_up.rearrange("(k p) f -> p k f", p=P))]
            for h in range(HALVES):
                r0 = h * F
                full = (FC - 1) * P
                shared += [(sd[:, h, 0:FC - 1, :], sw_down[r0:r0 + full, :].rearrange("(c p) d -> p c d", p=P)),
                           (sd[0:FROWS[-1], h, FC - 1, :], sw_down[r0 + full:r0 + F, :])]

            def load_job_x(t):
                if t >= 2:
                    sp.wait_ge(s["turned_x"], t - 1)
                sp.dma_start(x_job[:, t % 2, :], xn2_d[t * P:(t + 1) * P, :]).then_inc(s[f"xin{t % 2}"], 16)

            load_job_x(0)
            load_job_x(1)
            for dst, src in shared:
                sp.dma_start(dst, src).then_inc(s["shared_in"], 16)
            for e in range(E):
                full = (FC - 1) * P
                sp.dma_start(wg[:, e], w_gate[e].rearrange("(k p) f -> p k f", p=P)).then_inc(s["routed_in"], 16)
                sp.dma_start(wu[:, e], w_up[e].rearrange("(k p) f -> p k f", p=P)).then_inc(s["routed_in"], 16)
                sp.dma_start(wd[:, e, 0:FC - 1, :], w_down[e, 0:full, :].rearrange("(c p) d -> p c d", p=P))\
                  .then_inc(s["routed_in"], 16)
                sp.dma_start(wd[0:FROWS[-1], e, FC - 1, :], w_down[e, full:F, :]).then_inc(s["routed_in"], 16)
            for t in range(2, NT):
                load_job_x(t)
            for q in range(2):
                sp.wait_ge(s[f"yo{q}"], 16 * ((NT + JOBS - 1 - q) // 2 + 1))

        SHARED_DMAS = 2 + 2 * HALVES
        ROUTED_DMAS = 4 * E

        @block.gpsimd
        def _(pool):
            step = [0]

            def const(ins):
                step[0] += 1
                ins.then_inc(s["cst_a"], 1)
                pool.wait_ge(s["cst_a"], step[0])

            def band(ap, pattern, base, mult):
                const(pool.affine_select(out=ap, in_=ap, compare_op=ALU.is_ge, fill=0.0, base=base,
                                         pattern=pattern, channel_multiplier=mult))

            for g in range(P // DH):
                pool.dma_start(dec[g * DH:(g + 1) * DH, :], bass.AP(decay.tensor, g, [[0, DH], [P // DH, KC]]),
                               allow_slow_non_contiguous=True).then_inc(s["dec_in"], 16)
            const(pool.memset(ident[:, :], 0.0))
            const(pool.affine_select(out=ident[:, :], in_=ident[:, :], compare_op=ALU.not_equal, fill=1.0,
                                     base=0, pattern=[[-1, P]], channel_multiplier=1))
            const(pool.memset(neg_half[:, :], -0.5))
            pool.nop().then_inc(s["consts"], 1)

            def rstd_of(mv, ve, rs, gate, value, got, done):
                pool.wait_ge(s[gate], value)
                pool.tensor_scalar(ve, mv, LN_EPS, None, ALU.add).then_inc(s[got], 1)
                pool.wait_ge(s[got], value)
                pool.tensor_tensor(rs, ve, neg_half[:, :], ALU.pow).then_inc(s[done], 1)

            def rstd_1(t):
                b = t % 2
                rstd_of(mean_var[:, b, 1:2], var_eps[:, b:b + 1], rstd[:, b:b + 1], "var1", t + 1, "veps1", "rstd1")

            def rstd_2(t):
                b = t % 2
                rstd_of(mean_var2[:, b, 1:2], var_eps2[:, b:b + 1], rstd2[:, b:b + 1], "var2", t + 1, "veps2",
                        "rstd2_s")

            for t in range(TPB):
                rstd_1(t)
            for ap, pat in ((head_of, [[P, KC], [-DH, HEADS]]),):
                const(pool.memset(ap[:, :, :], 1.0))
                band(ap[:, :, :], pat, 0, 1)
                band(ap[:, :, :], [[-a, b] for a, b in pat], DH - 1, -1)
            const(pool.memset(of_head[:, :, :], 1.0))
            band(of_head[:, :, :], [[P, KC], [1, P]], 0, -DH)
            band(of_head[:, :, :], [[-P, KC], [-1, P]], DH - 1, DH)
            pool.nop().then_inc(s["consts"], 1)
            for n in range(NB + 2):
                for t in (2, 3):
                    if n >= 2:
                        rstd_2((n - 2) * TPB + t)
                if n + 1 < NB:
                    for t in range(TPB):
                        rstd_1((n + 1) * TPB + t)
                for t in (0, 1):
                    if 1 <= n <= NB:
                        rstd_2((n - 1) * TPB + t)
            pool.wait_ge(s["gate_mm"], NT)
            stores_done(pool)
            const(pool.memset(zeros[:, :], 0.0))
            for ap in (out, xn2_d):
                for a in range(8):
                    pool.dma_start(ap[T:ROWS, a * (D // 8):(a + 1) * (D // 8)], zeros[:, :])\
                        .then_inc(s["pad_out"], 16)
            const(pool.memset(ones[:, :], 1.0))
            const(pool.memset(tri[:, :], 1.0))
            band(tri[:, :], [[1, P]], -1, -1)
            const(pool.memset(not_first[:, :, :], 1.0))
            const(pool.memset(not_first[:, :, 0:1], 0.0))
            for ap, pat, b0, mult in ((iota_e, [[1, E]], 0, 0), (iota_j, [[1, JW]], 0, 0),
                                      (iota_p, [[1, P]], 0, 0), (token_1, [[P, NT]], 1, 1),
                                      (spare, [[0, 1]], T + 1, 1)):
                const(pool.iota(ap[:, :], pattern=pat, base=b0, channel_multiplier=mult,
                                allow_small_or_imprecise_dtypes=True))
            pool.nop().then_inc(s["cst_b"], 1)

            def prev_out(t):
                return s[f"yo{(t - 1) % 2}"], 16 * ((t - 1) // 2 + 1)

            def add_shared(t):
                pool.wait_ge(s["y_s"], t + 1)
                pool.dma_start(out[t * P:(t + 1) * P, :], y_job[:, t % 2, :], accum_op=ALU.add)\
                    .then_inc(s[f"yo{t % 2}"], 16)

            def gather(r, b):
                pool.tensor_copy(idx_in[:, b:b + 1], job_tok[:, bass.ds(r, 1)]).then_inc(s["idxg_s"], 1)
                seen, free = pool.to_reg(r + 1), pool.to_reg(NT + r - 1)
                pool.wait_ge(s["xn2_out0"], 8 * NT)
                pool.wait_ge(s["idxg_s"], seen)
                pool.wait_ge(s["turned_x"], free)
                pool.indirect_dma_start(x_job[:, b, :], None, xn2_d[:, :],
                                        bass.IndirectOffsetOnAxis(idx_in[:, b:b + 1], 0))\
                    .then_inc(s[f"gin{b}"], 16)

            def scatter(r, b):
                pool.wait_ge(s[f"yo{1 - b}"], 16 * (NT // 2) + 8 * (r + b))
                pool.tensor_copy(idx_out[:, b:b + 1], job_tok[:, bass.ds(r, 1)]).then_inc(s["idxs_s"], 1)
                seen, ready = pool.to_reg(r + 1), pool.to_reg(NT + r + 1)
                pool.wait_ge(s["x2_out0"], 8 * NT)
                pool.wait_ge(s["idxs_s"], seen)
                pool.wait_ge(s["y_s"], ready)
                pool.indirect_dma_start(out[:, :], bass.IndirectOffsetOnAxis(idx_out[:, b:b + 1], 0),
                                        y_job[:, b, :], None, compute_op=ALU.add).then_inc(s[f"yo{b}"], 16)

            for t in range(NT - 2):
                add_shared(t)
            pool.wait_ge(s["tables_s"], 1)
            pool.wait_ge(s["pad_out"], 16 * 16)
            gather(0, 0)
            gather(1, 1)
            add_shared(NT - 2)
            add_shared(NT - 1)
            with pool.Fori(0, JOBS // 2 - 1) as i:
                for b in range(2):
                    gather(2 * i + b + 2, b)
                    scatter(2 * i + b, b)
            r = 2 * (JOBS // 2 - 1)
            gather(r + 2, 0)
            scatter(r, 0)
            scatter(r + 1, 1)
            scatter(r + 2, 0)

        @block.scalar
        def _(act):
            act.wait_ge(s["dec_in"], 16 * (P // DH))
            act.activation(dec[:, :], dec[:, :], ACT.Exp, scale=-1.0).then_inc(s["dec_e"], 1)

            def hi_x(t):
                act.wait_ge(s["turned1"], t + 1)
                if t >= 2 * TPB:
                    act.wait_ge(s["q_mm"], KC * (t // TPB - 1))
                n, j = t // TPB, t % TPB
                act.copy(xnT_h[:, n % 2, :, j * P:(j + 1) * P], turn[:, :, :]).then_inc(s["hi1"], 1)

            def hi_w(k):
                if k < KC:
                    act.wait_ge(s["w_in"], 16 * (k + 1))
                    act.copy(wq_h[:, k, :], w_raw[:, :]).then_inc(s["w_hi"], 1)
                else:
                    act.wait_ge(s["w_out_in"], 16 * (k - KC + 1))
                    act.copy(wo_h[:, k - KC, :], w_raw[:, 0:D]).then_inc(s["w_hi"], 1)

            def phi_parts(n, c, which):
                i = n * KC + c
                item = k_item if which == 0 else q_item
                act.wait_ge(s["k_mm" if which == 0 else "q_mm"], i + 1)
                if i:
                    act.wait_ge(s["phik_s" if which == 0 else "phiq_s"], i)
                z = ring[item(n, c) % RING]
                act.activation(exp_z[:, which, :], z[:, :], ACT.Exp)
                act.activation(relu_z[:, which, :], z[:, :], ACT.Relu)\
                    .then_inc(s["k_act" if which == 0 else "q_act"], 1)

            def hi_a(n, c):
                i = n * KC + c
                act.wait_ge(s["a_s"], i + 1)
                if n:
                    act.wait_ge(s["out_mm"], n * TPB)
                act.copy(at_h[:, c, :], num[:, n % 2, c, :]).then_inc(s["ah_s"], 1)

            def move_xn2T(t):
                act.wait_ge(s["turned2"], t + 1)
                if t:
                    act.wait_ge(s["gate_mm"], t)
                act.copy(xn2T[:, :, :], turn[:, :, :]).then_inc(s["xn2T_s"], 1)

            hi_w(0)
            hi_x(0)
            hi_w(1)
            hi_x(1)
            hi_w(2)
            hi_x(2)
            hi_w(3)
            hi_x(3)
            for c in chunks:
                hi_w(KC + c)
            for n in blocks:
                moves = [(n - 2) * TPB + j for j in range(TPB)] if n >= 2 else []
                phi_parts(n, 0, 0)
                for t in moves[0:1]:
                    move_xn2T(t)
                phi_parts(n, 0, 1)
                for t in moves[1:2]:
                    move_xn2T(t)
                phi_parts(n, 1, 0)
                for t in moves[2:4]:
                    move_xn2T(t)
                if n:
                    for c in chunks:
                        hi_a(n - 1, c)
                phi_parts(n, 1, 1)
                for j in range(TPB):
                    if n + 1 < NB:
                        hi_x((n + 1) * TPB + j)
                    if j == 0:
                        phi_parts(n, 2, 0)
                    if j == 2:
                        phi_parts(n, 2, 1)
                phi_parts(n, 3, 0)
                phi_parts(n, 3, 1)
            for t in range((NB - 2) * TPB, (NB - 1) * TPB):
                move_xn2T(t)
            for c in chunks:
                hi_a(NB - 1, c)
            for t in range((NB - 1) * TPB, NT):
                move_xn2T(t)

            def move_xT(t, b):
                act.wait_ge(s["turned_x"], t + 1)
                act.copy(xT[:, b], turn_x[:, :, :]).then_inc(s["xT_s"], 1)

            def gate_silu(u, b, first=False):
                act.wait_ge(s["gu_mm"], u + 1)
                if not first:
                    act.wait_ge(s["hid_s"], u - 1)
                act.activation(silu[:, b, :], ps_g[b][:, 0:F], ACT.Silu).then_inc(s["silu_s"], 1)

            def move_y(t, b, first=False):
                act.wait_ge(s["y_mm"], t + 1)
                if not first:
                    act.wait_ge(s[f"yo{b}"], 8 * (t - b))
                act.copy(y_job[:, b, :], ps_y[b][:, :]).then_inc(s["y_s"], 1)

            act.wait_ge(s["gate_mm"], NT)
            stores_done(act)
            move_xT(0, 0)
            act.wait_ge(s["rt_exp_in"], 1)
            act.activation(tab_a[:, :, :], tab_a[:, :, :], ACT.Exp).then_inc(s["rt_exp"], 1)

            def two_tiles(i, first=False):
                u, t = 4 * i, 2 * i
                gate_silu(u + 1, 1, first)
                move_xT(t + 1, 1)
                gate_silu(u + 2, 0)
                move_y(t, 0, first)
                gate_silu(u + 3, 1)
                move_xT(t + 2, 0)
                gate_silu(u + 4, 0)
                move_y(t + 1, 1, first)

            gate_silu(0, 0, True)
            two_tiles(0, first=True)
            with act.Fori(1, NT // 2) as i:
                two_tiles(i)
            with act.Fori(0, JOBS // 2) as i:
                for b in (1, 2):
                    move_xT(NT + 2 * i + b, b % 2)
                    gate_silu(HALVES * NT + 2 * i + b, b % 2)

        @block.vector
        def _(dve):
            loc = [0]

            def link(ins):
                loc[0] += 1
                ins.then_inc(s["d_route"], 1)
                dve.wait_ge(s["d_route"], loc[0])

            dve.wait_ge(s["dec_e"], 1)
            dve.tensor_scalar(dec[:, :], dec[:, :], 1.0, None, ALU.add).then_inc(s["dec_1"], 1)
            dve.wait_ge(s["dec_1"], 1)
            dve.reciprocal(dec[:, :], dec[:, :]).then_inc(s["dec_ok"], 1)

            def stats_x(t):
                b = t % 2
                dve.wait_ge(*tile_sem("xl", t))
                if t >= 2:
                    dve.wait_ge(s["xn1"], t - 1)
                dve.bn_stats(stats[:, b, :], x_in[:, b, :]).then_inc(s["stat1"], 1)
                dve.wait_ge(s["stat1"], t + 1)
                dve.bn_aggr(mean_var[:, b, :], stats[:, b, :]).then_inc(s["var1"], 1)

            def norm_x(t):
                b = t % 2
                dve.wait_ge(s["var1"], t + 1)
                dve.wait_ge(s["rstd1"], t + 1)
                if t:
                    dve.wait_ge(s["turned1"], t)
                dve.tensor_scalar(xn[:, :], x_in[:, b, :], mean_var[:, b, 0:1], rstd[:, b:b + 1],
                                  ALU.subtract, ALU.mult).then_inc(s["xn1"], 1)

            def lo_x(t):
                n, j = t // TPB, t % TPB
                at = (slice(None), n % 2, slice(None), slice(j * P, (j + 1) * P))
                dve.wait_ge(s["hi1"], t + 1)
                dve.tensor_tensor(xnT_l[at], turn[:, :, :], xnT_h[at].bitcast(F32), ALU.subtract)\
                    .then_inc(s["lo1"], 1)

            def lo_w(k):
                dve.wait_ge(s["w_hi"], k + 1)
                if k < KC:
                    dve.tensor_tensor(wq_l[:, k, :], w_raw[:, :], wq_h[:, k, :].bitcast(F32), ALU.subtract)\
                        .then_inc(s["w_lo"], 1)
                else:
                    dve.tensor_tensor(wo_l[:, k - KC, :], w_raw[:, 0:D], wo_h[:, k - KC, :].bitcast(F32),
                                      ALU.subtract).then_inc(s["w_lo"], 1)

            def states(n, c):
                i = n * KC + c
                dcol = dec[:, c:c + 1].broadcast_to([P, BLK])
                if i:
                    for name in ("kv_s", "sk_s", "skv_s", "qk_s", "num_s"):
                        dve.wait_ge(s[name], i)
                    dve.wait_ge(s["carry_s"], 2 * i)
                dve.wait_ge(s["k_act"], i + 1)
                dve.scalar_tensor_tensor(out=phi_k[:, :], in0=exp_z[:, 0, :], scalar=1.0, in1=relu_z[:, 0, :],
                                         op0=ALU.min, op1=ALU.add).then_inc(s["phik_s"], 1)
                dve.wait_ge(s["phik_s"], i + 1)
                dve.wait_ge(s["v_mm"], i + 1)
                dve.tensor_tensor(kv[:, :], phi_k[:, :], ring[v_item(n, c) % RING][:, :], ALU.mult)\
                    .then_inc(s["kv_s"], 1)
                start = n % BPS == 0
                if not start:
                    dve.wait_ge(s["carry_s"], 2 * (i - KC + 1))
                dve.tensor_tensor_scan(run_k[:, :], dcol, phi_k[:, :], 0.0 if start else carry[:, 0, c:c + 1],
                                       ALU.mult, ALU.add).then_inc(s["sk_s"], 1)
                dve.wait_ge(s["kv_s"], i + 1)
                dve.tensor_tensor_scan(run_kv[:, :], dcol, kv[:, :], 0.0 if start else carry[:, 1, c:c + 1],
                                       ALU.mult, ALU.add).then_inc(s["skv_s"], 1)

            def query(n, c):
                i = n * KC + c
                dve.wait_ge(s["q_act"], i + 1)
                dve.scalar_tensor_tensor(out=phi_q[:, :], in0=exp_z[:, 1, :], scalar=1.0, in1=relu_z[:, 1, :],
                                         op0=ALU.min, op1=ALU.add).then_inc(s["phiq_s"], 1)
                dve.wait_ge(s["sk_s"], i + 1)
                dve.tensor_copy(carry[:, 0, c:c + 1], run_k[:, BLK - 1:BLK]).then_inc(s["carry_s"], 1)
                dve.wait_ge(s["phiq_s"], i + 1)
                if i >= 2:
                    dve.wait_ge(s["den_mm"], i - 1)
                dve.tensor_tensor(qk[:, c % 2, :], phi_q[:, :], run_k[:, :], ALU.mult).then_inc(s["qk_s"], 1)
                dve.wait_ge(s["skv_s"], i + 1)
                dve.tensor_copy(carry[:, 1, c:c + 1], run_kv[:, BLK - 1:BLK]).then_inc(s["carry_s"], 1)
                if n >= 2:
                    dve.wait_ge(s["al_s"], (n - 2) * KC + c + 1)
                    dve.wait_ge(s["ah_s"], (n - 2) * KC + c + 1)
                dve.tensor_tensor(num[:, n % 2, c, :], phi_q[:, :], run_kv[:, :], ALU.mult).then_inc(s["num_s"], 1)

            def denominators(n):
                dve.wait_ge(s["den_mm"], (n + 1) * KC)
                if n:
                    dve.wait_ge(s["rden_s"], n)
                dve.tensor_scalar(den[:, :], ps_den[0:HEADS, :], DEN_EPS, None, ALU.max).then_inc(s["den_max"], 1)
                dve.wait_ge(s["den_max"], n + 1)
                if n:
                    dve.wait_ge(s["ex_mm"], n * KC)
                dve.reciprocal(rden[:, :], den[:, :]).then_inc(s["rden_s"], 1)

            def divide(n):
                for c in chunks:
                    i = n * KC + c
                    dve.wait_ge(s["ex_mm"], i + 1)
                    dve.wait_ge(s["num_s"], i + 1)
                    a = num[:, n % 2, c, :]
                    dve.tensor_tensor(a, a, ring[items[(n, c, "ex")] % RING][:, :], ALU.mult).then_inc(s["a_s"], 1)

            def lo_a(n):
                for c in chunks:
                    i = n * KC + c
                    dve.wait_ge(s["ah_s"], i + 1)
                    if n:
                        dve.wait_ge(s["out_mm"], n * TPB)
                    dve.tensor_tensor(at_l[:, c, :], num[:, n % 2, c, :], at_h[:, c, :].bitcast(F32), ALU.subtract)\
                        .then_inc(s["al_s"], 1)

            def residual(t):
                b = t % 2
                dve.wait_ge(s["out_mm"], t + 1)
                dve.wait_ge(*tile_sem("xr", t))
                if t >= 2:
                    dve.wait_ge(s[f"x2_out{b}"], 16 * (t // 2))
                    dve.wait_ge(s["xn2_s"], t - 1)
                n, j = t // TPB, t % TPB
                dve.tensor_tensor(x2[:, b, :], ring[items[(n, j, "out")] % RING][:, :], x_res[:, b, :], ALU.add)\
                    .then_inc(s["x2_s"], 1)
                dve.wait_ge(s["x2_s"], t + 1)
                dve.bn_stats(stats2[:, b, :], x2[:, b, :]).then_inc(s["stat2"], 1)
                dve.wait_ge(s["stat2"], t + 1)
                dve.bn_aggr(mean_var2[:, b, :], stats2[:, b, :]).then_inc(s["var2"], 1)

            def norm_2(t):
                b = t % 2
                dve.wait_ge(s["var2"], t + 1)
                dve.wait_ge(s["rstd2_s"], t + 1)
                if t >= 2:
                    dve.wait_ge(s[f"xn2_out{b}"], 16 * (t // 2))
                    dve.wait_ge(s["turned2"], t - 1)
                dve.tensor_scalar(xn2[:, b, :], x2[:, b, :], mean_var2[:, b, 0:1], rstd2[:, b:b + 1],
                                  ALU.subtract, ALU.mult).then_inc(s["xn2_s"], 1)

            stats_x(0)
            stats_x(1)
            norm_x(0)
            lo_w(0)
            lo_x(0)
            norm_x(1)
            stats_x(2)
            lo_w(1)
            lo_x(1)
            norm_x(2)
            stats_x(3)
            lo_w(2)
            lo_x(2)
            norm_x(3)
            lo_w(3)
            lo_x(3)
            for c in chunks:
                lo_w(KC + c)
            for n in blocks:
                def before(step, *args):
                    if n:
                        step(n - 1, *args)

                def tile_before(step, j, ago=1):
                    if n >= ago:
                        step((n - ago) * TPB + j)

                def next_x(step, j):
                    if n + 1 < NB:
                        step((n + 1) * TPB + j)

                before(denominators)
                states(n, 0)
                tile_before(norm_2, 2, 2)
                tile_before(residual, 3, 2)
                query(n, 0)
                tile_before(norm_2, 3, 2)
                next_x(stats_x, 0)
                next_x(stats_x, 1)
                states(n, 1)
                next_x(norm_x, 0)
                before(divide)
                query(n, 1)
                before(lo_a)
                next_x(lo_x, 0)
                next_x(norm_x, 1)
                next_x(stats_x, 2)
                states(n, 2)
                next_x(lo_x, 1)
                next_x(norm_x, 2)
                next_x(stats_x, 3)
                next_x(lo_x, 2)
                next_x(norm_x, 3)
                query(n, 2)
                next_x(lo_x, 3)
                tile_before(residual, 0)
                states(n, 3)
                tile_before(norm_2, 0)
                tile_before(residual, 1)
                query(n, 3)
                tile_before(norm_2, 1)
                tile_before(residual, 2)
            t = (NB - 2) * TPB
            norm_2(t + 2)
            residual(t + 3)
            norm_2(t + 3)
            denominators(NB - 1)
            divide(NB - 1)
            lo_a(NB - 1)
            t += TPB
            residual(t)
            for j in range(1, TPB):
                residual(t + j)
                norm_2(t + j - 1)
            norm_2(NT - 1)
            dve.wait_ge(s["gate_mm"], NT)
            dve.tensor_copy(logits[:, :, :], ps_gate[:, :, 0:E]).then_inc(s["logit_s"], 1)
            stores_done(dve)
            dve.wait_ge(s["logit_s"], 1)

            wide = lambda ap: ap.unsqueeze(2).broadcast_to([P, NT, E])
            link(dve.tensor_reduce(row_a[:, :], logits[:, :, :], AX_X, ALU.max))
            dve.tensor_tensor(tab_a[:, :, :], logits[:, :, :], wide(row_a[:, :]), ALU.subtract)\
                .then_inc(s["rt_exp_in"], 1)
            dve.wait_ge(s["rt_exp"], 1)
            link(dve.tensor_reduce(row_a[:, :], tab_a[:, :, :], AX_X, ALU.add))
            link(dve.reciprocal(row_b[:, :], row_a[:, :]))
            link(dve.tensor_tensor(score[:, :, :], tab_a[:, :, :], wide(row_b[:, :]), ALU.mult))
            for t in range(NT):
                ins = dve.max(top[:, t, :], score[:, t, :])
            link(ins)
            for t in range(NT):
                ins = dve.max_index(top_i[:, t, :], top[:, t, :], score[:, t, :])
            link(ins)
            dve.wait_ge(s["cst_b"], 1)
            link(dve.tensor_copy(top_f[:, :, :], top_i[:, :, 0:TOPK].rearrange("p t k -> p k t")))
            over_t = iota_e[:, :].unsqueeze(1).broadcast_to([P, NT, E])
            for k in range(TOPK):
                ins = dve.tensor_tensor(pick[:, k], wide(top_f[:, k, :]), over_t, ALU.is_equal)
            link(ins)
            dve.tensor_tensor(picked[:, :, :], pick[:, 0], pick[:, 1], ALU.add).then_inc(s["picked_s"], 1)
            dve.wait_ge(s["rank_mm"], 1)
            ranks = ps_rank[:, 0:P].rearrange("p (t e) -> p t e", e=E)
            totals = ps_rank[:, P:2 * P].rearrange("p (t e) -> p e t", e=E)
            link(dve.tensor_copy(count[:, :, :], totals))
            flat = lambda ap: ap.rearrange("p e t -> p (e t)")
            link(dve.tensor_tensor_scan(flat(upto[:, :, :]), flat(not_first[:, :, :]), flat(count[:, :, :]), 0.0,
                                        ALU.mult, ALU.add))
            link(dve.tensor_scalar(jobs_i[:, :], upto[:, :, NT - 1], float(P - 1), None, ALU.add))
            link(dve.tensor_scalar(jobs_i[:, :], jobs_i[:, :], 7, None, ALU.arith_shift_right))
            link(dve.tensor_copy(jobs_f[:, :], jobs_i[:, :]))
            link(dve.tensor_tensor_scan(jobs_end[:, :], ones[:, 0:E], jobs_f[:, :], 0.0, ALU.mult, ALU.add))
            link(dve.tensor_tensor(jobs_beg[:, :], jobs_end[:, :], jobs_f[:, :], ALU.subtract))
            link(dve.tensor_tensor(base[:, :, :], upto[:, :, :], count[:, :, :], ALU.subtract))
            link(dve.tensor_scalar(jobs_beg[:, :], jobs_beg[:, :], float(P), None, ALU.mult))
            link(dve.tensor_tensor(base[:, :, :], base[:, :, :],
                                   jobs_beg[:, :].unsqueeze(2).broadcast_to([P, E, NT]), ALU.add))
            link(dve.tensor_tensor(slot_e[:, :, :], ranks, base[:, :, :].rearrange("p e t -> p t e"), ALU.add))
            for k in range(TOPK):
                link(dve.tensor_tensor(tab_a[:, :, :], slot_e[:, :, :], pick[:, k], ALU.mult))
                link(dve.tensor_reduce(slot_f[:, k, :], tab_a[:, :, :], AX_X, ALU.add))
            link(dve.tensor_copy(slot_i[:, :], slot_f[:, :, :].rearrange("p k t -> p (k t)")))
            link(dve.tensor_scalar(slot_ji[:, :], slot_i[:, :], 7, None, ALU.arith_shift_right))
            link(dve.tensor_scalar(slot_pi[:, :], slot_i[:, :], P - 1, None, ALU.bitwise_and))
            link(dve.tensor_copy(slot_j[:, :], slot_ji[:, :]))
            link(dve.tensor_copy(slot_p[:, :], slot_pi[:, :]))
            link(dve.tensor_tensor(past[:, :, :], iota_j[:, :].unsqueeze(2).broadcast_to([P, JW, E]),
                                   jobs_end[:, :].unsqueeze(1).broadcast_to([P, JW, E]), ALU.is_ge))
            link(dve.tensor_reduce(job_ef[:, :], past[:, :, :], AX_X, ALU.add))
            link(dve.tensor_scalar(job_e[:, :], job_ef[:, :], float(E - 1), None, ALU.min))
            for m in range(TOPK * NT):
                k, t = m // NT, m % NT
                if m >= 2:
                    dve.wait_ge(s["acc_mm"], m - 1)
                dve.tensor_scalar(hot_p[:, m % 2, :], iota_p[:, :], slot_p[:, m:m + 1], None, ALU.is_equal)
                dve.tensor_scalar(hot_j[:, m % 2, 0, :], iota_j[:, :], slot_j[:, m:m + 1], token_1[:, t:t + 1],
                                  ALU.is_equal, ALU.mult)
                dve.tensor_scalar(hot_j[:, m % 2, 1, :], iota_j[:, :], slot_j[:, m:m + 1], top[:, t, k:k + 1],
                                  ALU.is_equal, ALU.mult).then_inc(s["hot_s"], 1)
            dve.wait_ge(s["acc_mm"], TOPK * NT)
            link(dve.tensor_copy(job_tok1[:, :], ps_acc[:, 0:JW]))
            link(dve.tensor_copy(job_w[:, :], ps_acc[:, JW:2 * JW]))
            link(dve.tensor_scalar(job_pad[:, :], job_tok1[:, :], 0.0, spare[:, 0:1], ALU.is_equal, ALU.mult))
            dve.scalar_tensor_tensor(out=job_tok[:, :], in0=job_tok1[:, :], scalar=-1.0, in1=job_pad[:, :],
                                     op0=ALU.add, op1=ALU.add).then_inc(s["tables_s"], 1)
            dve.wait_ge(s["tables_s"], 1)

            def hidden(u, b, first=False):
                dve.wait_ge(s["silu_s"], u + 1)
                if not first:
                    dve.wait_ge(s["turned_h"], u - 1)
                dve.tensor_tensor(hid[:, b, :], ps_u[b][:, 0:F], silu[:, b, :], ALU.mult).then_inc(s["hid_s"], 1)

            def move_hidT(u, b):
                dve.wait_ge(s["turned_h"], u + 1)
                for c, rows in enumerate(FROWS):
                    pass
                dve.tensor_copy(hidT[:, b, 0:FC - 1, :], turn_h[:, 0:FC - 1, :])
                dve.tensor_copy(hidT[0:FROWS[-1], b, FC - 1, :], turn_h[0:FROWS[-1], FC - 1, :])\
                    .then_inc(s["hidT_s"], 1)

            def weigh_y(r, b):
                t = NT + r
                dve.wait_ge(s["y_mm"], t + 1)
                dve.wait_ge(s[f"yo{b}"], 8 * (t - b))
                dve.tensor_scalar(y_job[:, b, :], ps_y[b][:, :], job_w[:, bass.ds(r, 1)], None, ALU.mult)\
                    .then_inc(s["y_s"], 1)

            def four(u, first=False):
                hidden(u + 1, 1, first)
                move_hidT(u, 0)
                hidden(u + 2, 0)
                move_hidT(u + 1, 1)
                hidden(u + 3, 1)
                move_hidT(u + 2, 0)

            hidden(0, 0, True)
            four(0, True)
            with dve.Fori(1, NT // 2) as i:
                hidden(4 * i, 0)
                move_hidT(4 * i - 1, 1)
                four(4 * i)
            R0 = HALVES * NT
            hidden(R0, 0)
            move_hidT(R0 - 1, 1)
            with dve.Fori(0, JOBS // 2) as i:
                hidden(R0 + 2 * i + 1, 1)
                move_hidT(R0 + 2 * i, 0)
                weigh_y(2 * i, 0)
                hidden(R0 + 2 * i + 2, 0)
                move_hidT(R0 + 2 * i + 1, 1)
                weigh_y(2 * i + 1, 1)
            move_hidT(R0 + JOBS - 1, 0)
            weigh_y(JOBS - 1, 0)

_INS = ['L0_attn_x', 'L0_attn_w_qkv', 'L0_attn_w_out', 'L0_attn_decay_param', 'L0_ffn_gate_w', 'L0_ffn_w_gate',
        'L0_ffn_w_up', 'L0_ffn_w_down', 'L0_ffn_sw_gate', 'L0_ffn_sw_up', 'L0_ffn_sw_down']


def kernel(**inputs):
    import numpy as _np
    import concourse.bacc as _bacc
    from concourse import mybir as _mybir
    from concourse.bass_utils import run_bass_kernel_spmd as _run

    nc = _bacc.Bacc("TRN2", target_bir_lowering=False, num_devices=1)
    arrays, args = {}, []
    for name in _INS:
        a = _np.ascontiguousarray(inputs[name])
        arrays[f"in_{name}_dram"] = a
        args.append(nc.dram_tensor(f"in_{name}_dram", a.shape, _mybir.dt.from_np(a.dtype), kind="ExternalInput").ap())
    B, S, D = inputs['L0_attn_x'].shape
    args.append(nc.dram_tensor("out_dram", (B * S + 128, D), _mybir.dt.float32, kind="ExternalOutput").ap())
    preln_decay_attention_moe(nc, *args)
    r = _run(nc, [arrays], core_ids=[0])
    return r.results[0]["out_dram"][:B * S].reshape(B, S, D)
```

```python
from contextlib import ExitStack

import concourse.bass as bass
from concourse import mybir

P = 128
F32 = mybir.dt.float32
F32R = mybir.dt.float32r
F16 = mybir.dt.float16
BF16 = mybir.dt.bfloat16
I32 = mybir.dt.int32
U32 = mybir.dt.uint32
ALU = mybir.AluOpType
ACT = mybir.ActivationFunctionType
AX_X = mybir.AxisListType.X

LN_EPS = 1e-5
DEN_EPS = 1e-6
HID_SCALE = 2.0 ** -23
LN_SCALE = 2.0 ** 11


def preln_decay_attention_moe(nc, x, w_qkv, w_out, decay, gate_w, w_gate, w_up, w_down,
                              sw_gate, sw_up, sw_down, out):
    B, S, D = x.shape
    T = B * S
    HEADS = decay.shape[0]
    DH = D // HEADS
    E, _, F = w_gate.shape
    KC = D // P
    NT = T // P
    BLK = 512
    TPB = BLK // P
    NB = T // BLK
    BPS = S // BLK
    HALVES = sw_gate.shape[1] // F
    assert HALVES == 2 and NT % 4 == 0 and D == BLK
    FC = (F + P - 1) // P
    FCOL = [P * c for c in range(FC - 1)] + [F - P]
    OVER = P * FC - F
    TOPK = 2
    JOBS = (TOPK * T - E) // P + E
    JOBS -= 1 if (TOPK * T + E * (P - 1)) // P < JOBS else 0
    JW = JOBS + JOBS % 2
    ROWS = T + P

    xf = x.rearrange("b s d -> (b s) d")
    xn2_d = nc.dram_tensor("xn2_scratch", [ROWS, D], F32, kind="Internal").ap()

    with ExitStack() as ctx:
        def sb(name, shape, dt=F32, stack=ctx):
            return stack.enter_context(nc.sbuf_tensor(name, shape, dt))

        def psum(name, shape, dt=F32, stack=ctx):
            return stack.enter_context(nc.psum_tensor(name, shape, dt))

        def sem(name):
            return ctx.enter_context(nc.semaphore(name))

        ident = sb("ident", [P, P])
        GU = KC * F
        DN = FC * D
        sg = sb("sg", [P, 2, GU])
        su = sb("su", [P, 2, GU])
        sd = sb("sd", [P, HALVES, DN])
        planes = sb("planes", [P, 2, DN], F16)
        apart = ExitStack()
        squares = sb("squares", [P, DN], BF16, apart)
        apart.close()
        xn2T_l = sb("xn2T_l", [P, KC, P], F32R)
        gw = sb("gw", [P, KC, E])
        sb("squares_end", [P, DN // 2 - KC * (P + E)])
        ones_h = sb("ones_h", [P, P], BF16)
        SETS = E + 1
        part_max = sb("part_max", [P, 3, 2])
        col_max = sb("col_max", [P, SETS, 3])
        half_exp = sb("half_exp", [P, SETS, 3], I32)
        scale = sb("scale", [P, SETS, 3])
        unscale = sb("unscale", [P, SETS, 3])
        gw_h = sb("gw_h", [P, KC, E], F32R)
        gw_l = sb("gw_l", [P, KC, E], F32R)
        silu_scale = sb("silu_scale", [P, SETS])
        hid_scale = sb("hid_scale", [P, SETS])
        y_scale = sb("y_scale", [P, SETS])
        x_in = sb("x_in", [P, 2, D])
        x_job = x_in
        assert 3 * D == DN
        w_raw = planes[:, :, :].rearrange("p a n -> p (a n)").bitcast(F32)
        attn = ExitStack()
        asb = lambda name, shape, dt=F32: sb(name, shape, dt, attn)
        wq_h = asb("wq_h", [P, KC, 3 * D], F32R)
        wq_l = asb("wq_l", [P, KC, 3 * D], F32R)
        wo_h = asb("wo_h", [P, KC, D], F32R)
        wo_l = asb("wo_l", [P, KC, D], F32R)
        head_of = asb("head_of", [P, KC, HEADS])
        of_head = asb("of_head", [HEADS, KC, P])
        dec = asb("dec", [P, KC])
        carry = asb("carry", [P, 2, KC])
        x_res = asb("x_res", [P, 2, D])
        stats = asb("stats", [P, 2, 6])
        mean_var = asb("mean_var", [P, 2, 2])
        var_eps = asb("var_eps", [P, 2])
        rstd = asb("rstd", [P, 2])
        stats2 = asb("stats2", [P, 2, 6])
        mean_var2 = asb("mean_var2", [P, 2, 2])
        var_eps2 = asb("var_eps2", [P, 2])
        rstd2 = asb("rstd2", [P, 2])
        neg_half = asb("neg_half", [P, 1])
        xn = asb("xn", [P, D])
        xnT_h = asb("xnT_h", [P, 2, KC, BLK], F32R)
        xnT_l = asb("xnT_l", [P, 2, KC, BLK], F32R)
        exp_z = asb("exp_z", [P, 2, BLK])
        relu_z = asb("relu_z", [P, 2, BLK])
        phi_q = asb("phi_q", [P, BLK])
        run_k = asb("run_k", [P, BLK])
        run_kv = asb("run_kv", [P, BLK])
        qk = asb("qk", [P, 2, BLK])
        whole = ExitStack()
        num = sb("num", [P, 2, KC, BLK], stack=whole)
        whole.close()
        at_l = asb("at_l", [P, 2, KC, BLK], F32R)
        den = asb("den", [HEADS, BLK])
        at_h = asb("at_h", [P, KC, BLK], F32R)
        x2 = asb("x2", [P, 2, D])
        xn2 = asb("xn2", [P, 2, D])
        xn2T_h = asb("xn2T_h", [P, KC, P], F32R)
        attn.close()
        moe = ExitStack()
        msb = lambda name, shape, dt=F32: sb(name, shape, dt, moe)
        logits = msb("logits", [P, NT, E])
        xT = msb("xT", [P, 2, 2, KC, P], F16)
        silu = msb("silu", [P, F])
        hid = msb("hid", [P, F])
        hidT = msb("hidT", [P, 2, FC, P], F16)
        y_job = msb("y_job", [P, 2, D])
        wg = msb("wg", [P, E, GU])
        wu = msb("wu", [P, E, GU])
        wd = msb("wd", [P, E, DN])
        tri = msb("tri", [P, P])
        ones = msb("ones", [P, P])
        zeros = msb("zeros", [P, D // 8])
        iota_e = msb("iota_e", [P, E])
        iota_j = msb("iota_j", [P, JW])
        iota_p = msb("iota_p", [P, P])
        token_1 = msb("token_1", [P, TOPK, NT])
        choice_w = msb("choice_w", [P, TOPK, NT])
        choice_h = msb("choice_h", [P, TOPK, NT], F32R)
        choice_l = msb("choice_l", [P, TOPK, NT])
        spare = msb("spare", [P, 1])
        slot_f = msb("slot_f", [P, TOPK, NT])
        slot_i = msb("slot_i", [P, TOPK * NT], I32)
        slot_ji = msb("slot_ji", [P, TOPK * NT], I32)
        slot_pi = msb("slot_pi", [P, TOPK * NT], I32)
        slot_j = msb("slot_j", [P, TOPK * NT])
        slot_p = msb("slot_p", [P, TOPK * NT])
        top_f = msb("top_f", [P, TOPK, NT])
        row_a = msb("row_a", [P, NT])
        row_b = msb("row_b", [P, NT])
        jobs_f = msb("jobs_f", [P, E])
        jobs_i = msb("jobs_i", [P, E], I32)
        jobs_end = msb("jobs_end", [P, E])
        jobs_beg = msb("jobs_beg", [P, E])
        early = ExitStack()
        esb = lambda name, shape, dt=F32: sb(name, shape, dt, early)
        tab_a = esb("tab_a", [P, NT, E])
        score = esb("score", [P, NT, E])
        top = esb("top", [P, NT, 8])
        top_i = esb("top_i", [P, NT, 8], U32)
        pick = esb("pick", [P, TOPK, NT, E])
        picked = esb("picked", [P, NT, E])
        not_first = esb("not_first", [P, E, NT])
        count = esb("count", [P, E, NT])
        upto = esb("upto", [P, E, NT])
        base = esb("base", [P, E, NT])
        slot_e = esb("slot_e", [P, NT, E])
        early.close()
        hots = ExitStack()
        past = sb("past", [P, JW, E], stack=hots)
        job_is = sb("job_is", [P, JW, E], stack=hots)
        hots.close()
        hot_p = msb("hot_p", [P, 4, P], F32R)
        hot_j = msb("hot_j", [P, 4, 3, JW], F32R)
        job_ef = msb("job_ef", [P, JW])
        job_ec = msb("job_ec", [P, JW])
        job_e = msb("job_e", [P, JW], I32)
        job_tok1 = msb("job_tok1", [P, JW])
        job_pad = msb("job_pad", [P, JW])
        job_tok = msb("job_tok", [P, JW], I32)
        job_w = msb("job_w", [P, JW])
        job_silu = msb("job_silu", [P, JW])
        job_hid = msb("job_hid", [P, JW])
        job_y = msb("job_y", [P, JW])
        idx_in = msb("idx_in", [P, 2], I32)
        idx_out = msb("idx_out", [P, 2], I32)
        moe.close()

        pa = ExitStack()
        turn = psum("turn", [P, KC, P], stack=pa)
        RING = 5
        ring = [psum(f"ring{i}", [P, BLK], stack=pa) for i in range(RING)]
        ps_den = psum("ps_den", [P, BLK], stack=pa)
        ps_gate = psum("ps_gate", [P, 512], stack=pa)
        pa.close()
        pm = ExitStack()
        turn_x = psum("turn_x", [P, KC, P], stack=pm)
        ps_g = psum("ps_g", [P, 512], stack=pm)
        ps_y = psum("ps_y", [P, D], stack=pm)
        turn_h = psum("turn_h", [P, 4, P], stack=pm)
        ps_u = psum("ps_u", [P, 512], stack=pm)
        ps_rt = psum("ps_rt", [P, 512], stack=pm)
        ps_norm = psum("ps_norm", [P, 512], stack=pm)
        pm.close()

        names = """wk0 wk1 wk2 wk3 wk4 wk5 wk6 wk7 w_in0 w_in1 w_in2 w_hi w_lo consts dec_in dec_e dec_1 dec_ok gw_in
            xl0 xl1 xs0 xs1 stat1 var1 veps1 rstd1 xn1 turned1 hi1 lo1 k_mm v_mm q_mm k_act q_act
            phik_s kv_s sk_s skv_s carry_s phiq_s qk_s num_s den_mm den_max rden_s ex_mm a_s ah_s
            al_s out_mm xr0 xr1 x2_s stat2 var2 veps2 rstd2_s xn2_s turned2 xn2Th_s xn2T_s gw_h_s
            gw_l_s gate_mm logit_s x2_out0 x2_out1 xn2_out0 xn2_out1 pad_out cst_a cst_b shared_in
            over_0 w0 w1 w2 w3 w4 w5 w6 w7 square_s fold_s norm_mm max_s set_s upper_s split_s
            rest_s d_set d_route rt_exp rt_exp_in picked_s hot_s route_mm tables_s xin0 xin1 gin0
            gin1 turned_x xTh_s xT_s g_mm u_mm silu_s hid_s turned_h hidTh_s hidT_s y_mm y_s idxg_s
            idxs_s yo0 yo1""".split()
        s = {n: sem(n) for n in names}
        block = ctx.enter_context(nc.Block())

        blocks = range(NB)
        chunks = range(KC)
        ps_rank, ps_acc = ps_rt[:, 0:2 * P], ps_rt[:, 2 * P:2 * P + 3 * JW]
        SHARED_DMAS = 2 + 2 * HALVES
        FIRST_TABLE = 4
        LAST_TABLE = FIRST_TABLE + TOPK * NT // 4 - 1
        table_choices = lambda u: [m for m in (2 * (u - 2 * FIRST_TABLE), 2 * (u - 2 * FIRST_TABLE) + 1)
                                   if 0 <= m < TOPK * NT]
        assert JOBS % 2 == 1 and LAST_TABLE < NT - 2
        pieces = [(E, kind, h, w[:, h]) for kind, w in enumerate((sg, su, sd)) for h in range(2)]
        SHARED_PIECES = len(pieces)
        pieces += [(e, kind, 0, w[:, e]) for e in range(E) for kind, w in enumerate((wg, wu, wd))]
        SPLIT_UNIT = 7
        NORM_UNIT = 2
        assert SPLIT_UNIT >= NORM_UNIT + 5 and SPLIT_UNIT + 3 * E <= HALVES * NT - 1
        norm_unit = lambda u: SHARED_PIECES + u - NORM_UNIT if NORM_UNIT <= u < NORM_UNIT + 3 * E else None

        def planes_of(n):
            return planes[:, :, :].rearrange("p a n -> p (a n)")[:, 0:2 * n].rearrange("p (a n) -> p a n", a=2)

        def norms_of(m):
            n = pieces[m][3].shape[1] // 4
            return ps_gate[:, P:P + n] if m < SHARED_PIECES else ps_norm[:, 0:n]

        FREE_PARTS = 2 * KC
        raw = lambda m: (num[:, m // KC, m % KC, :] if m < FREE_PARTS else
                         w_raw[:, ((m - FREE_PARTS) % 3) * D:((m - FREE_PARTS) % 3 + 1) * D])
        raw_in = lambda m: ((s[f"wk{m}"], 16) if m < FREE_PARTS else
                            (s[f"w_in{(m - FREE_PARTS) % 3}"], 16 * ((m - FREE_PARTS) // 3 + 1)))
        part_cols = lambda m: slice((1, 2, 0)[m // KC] * D, ((1, 2, 0)[m // KC] + 1) * D)
        QKV_PARTS = 3 * KC
        PARTS = QKV_PARTS + KC

        def part_of(m, qkv, outer):
            return qkv[:, m % KC, part_cols(m)] if m < QKV_PARTS else outer[:, m % KC, :]

        def x_rows(t):
            return (x_res if t in (2, 3) else x_in)[:, t % 2, :]

        def x_loaded(t):
            return (s[f"xs{t % 2}"], 16) if t in (2, 3) else (s[f"xl{t % 2}"], 16 * (t // 2 + (t < 2)))

        def turned_x(t):
            return ps_den[:, :].rearrange("p (k q) -> p k q", k=KC) if t < TPB and t % 2 else turn[:, :, :]

        NORM_STEP = 1
        SPLIT_STEP = 9
        assert NT * E <= P and NORM_STEP + SHARED_PIECES < 2 * KC < SPLIT_STEP <= NB * KC - SHARED_PIECES

        items = {}
        k_item = lambda n, c: items[(n, c, "k")]
        q_item = lambda n, c: items[(n, c, "q")]
        v_item = lambda n, c: items[(n, c, "v")]
        release = []

        def bank(eng, freed_by, value):
            m = len(release)
            if m >= RING:
                eng.wait_ge(*release[m - RING])
            release.append((s[freed_by], value))
            return ring[m % RING]

        tile_sem = lambda pair, t: (s[f"{pair}{t % 2}"], 16 * (t // 2 + 1))

        def stores_done(eng):
            for name in ("x2_out0", "x2_out1", "xn2_out0", "xn2_out1"):
                eng.wait_ge(s[name], 8 * NT)

        @block.tensor
        def _(pe):
            def split_product(ps, pairs):
                steps = []
                for (ah, al), (bh, bl) in pairs:
                    steps += [(ah, bh), (ah, bl), (al, bh)]
                for i, (a, b) in enumerate(steps):
                    ins = pe.matmul(ps, a, b, start=(i == 0), stop=(i == len(steps) - 1))
                return ins

            def column_norms(m):
                x, kind, h, w = pieces[m]
                pe.wait_ge(s["fold_s"], m + 1)
                if m:
                    pe.wait_ge(s["max_s"], m)
                n = w.shape[1] // 4
                for k in range(2):
                    ins = pe.matmul(norms_of(m), ones_h[:, :], squares[:, k * n:(k + 1) * n],
                                    start=(k == 0), stop=(k == 1))
                ins.then_inc(s["norm_mm"], 1)

            turned = []

            def turn_free():
                if turned:
                    pe.wait_ge(*turned[-1])

            def turn_x1(t):
                pe.wait_ge(s["xn1"], t + 1)
                if t >= TPB:
                    turn_free()
                elif t >= 2:
                    pe.wait_ge(s["lo1"], t - 1)
                turned.append((s["lo1"], t + 1))
                for k in chunks:
                    ins = pe.transpose(turned_x(t)[:, k, :], xn[:, k * P:(k + 1) * P], ident[:, :])
                ins.then_inc(s["turned1"], 1)

            def project(n, c, z):
                if n == 0 and c == 0:
                    pe.wait_ge(s["w_lo"], KC * {1: 1, 2: 2, 0: 3}[z])
                i = n * KC + c
                name, freed = {0: ("q", "q_act"), 1: ("k", "k_act"), 2: ("v", "kv_s")}[z]
                items[(n, c, name)] = len(release)
                ps = bank(pe, freed, i + 1)
                pairs = []
                for k in chunks:
                    cols = slice(z * D + c * P, z * D + (c + 1) * P)
                    pairs.append(((wq_h[:, k, cols], wq_l[:, k, cols]), (xnT_h[:, n % 2, k, :], xnT_l[:, n % 2, k, :])))
                split_product(ps[:, :], pairs).then_inc(s[name + "_mm"], 1)

            def sum_heads(n, c):
                i = n * KC + c
                if i == 0:
                    pe.wait_ge(s["consts"], 2)
                pe.wait_ge(s["qk_s"], i + 1)
                if n and c == 0:
                    pe.wait_ge(s["den_max"], n)
                pe.matmul(ps_den[0:HEADS, :], head_of[:, c, :], qk[:, c % 2, :], start=(c == 0), stop=(c == KC - 1))\
                    .then_inc(s["den_mm"], 1)

            def expand(n):
                pe.wait_ge(s["rden_s"], n + 1)
                for c in chunks:
                    items[(n, c, "ex")] = len(release)
                    ps = bank(pe, "a_s", n * KC + c + 1)
                    pe.matmul(ps[:, :], of_head[:, c, :], den[:, :], start=True, stop=True).then_inc(s["ex_mm"], 1)

            def output(n, j):
                pe.wait_ge(s["al_s"], (n + 1) * KC)
                if n == 0 and j == 0:
                    pe.wait_ge(s["w_lo"], PARTS)
                items[(n, j, "out")] = len(release)
                ps = bank(pe, "x2_s", n * TPB + j + 1)
                tok = slice(j * P, (j + 1) * P)
                split_product(ps[:, :], [((at_h[:, k, tok], at_l[:, n % 2, k, tok]), (wo_h[:, k, :], wo_l[:, k, :]))
                                         for k in chunks]).then_inc(s["out_mm"], 1)

            def turn_x2(t):
                pe.wait_ge(s["xn2_s"], t + 1)
                turn_free()
                turned.append((s["xn2T_s"], t + 1))
                for k in chunks:
                    ins = pe.transpose(turn[:, k, :], xn2[:, t % 2, k * P:(k + 1) * P], ident[:, :])
                ins.then_inc(s["turned2"], 1)

            def gate(t):
                if t == 0:
                    pe.wait_ge(s["gw_l_s"], 1)
                    pe.wait_ge(s["max_s"], SHARED_PIECES)
                pe.wait_ge(s["xn2T_s"], t + 1)
                ins = split_product(ps_gate[:, t * E:(t + 1) * E],
                                    [((xn2T_h[:, k, :], xn2T_l[:, k, :]), (gw_h[:, k, :], gw_l[:, k, :]))
                                     for k in chunks])
                ins.then_inc(s["gate_mm"], 1)

            def turn_job(t, b, sem_in, n_in, first=False):
                pe.wait_ge(s[f"{sem_in}{b}"], 8 * (n_in - b) + 16)
                if not first:
                    pe.wait_ge(s["xT_s"], t)
                for k in chunks:
                    ins = pe.transpose(turn_x[:, k, :], x_job[:, b, k * P:(k + 1) * P], ident[:, :])
                ins.then_inc(s["turned_x"], 1)

            def turn_tile(t, b, first=False):
                turn_job(t, b, "xin", t, first)

            def turn_gathered(r, b):
                turn_job(NT + r, b, "gin", r)

            def product(ps, a, w, n, start, stop):
                steps = [(i, j, k) for k in range(n) for i, j in ((0, 0), (0, 1), (1, 0))]
                for q, (i, j, k) in enumerate(steps):
                    ins = pe.matmul(ps, a[i][:, k, :], w(j, k), start=(start and q == 0),
                                    stop=(stop and q == len(steps) - 1))
                return ins

            def gate_product(u, t, tb, w, first=False):
                pe.wait_ge(s["xT_s"], t + 1)
                if not first:
                    pe.wait_ge(s["silu_s"], u)
                product(ps_g[:, 0:F], [xT[:, tb, h] for h in range(2)], w, KC, True, True).then_inc(s["g_mm"], 1)

            def up_product(u, tb, w, first=False):
                if not first:
                    pe.wait_ge(s["hid_s"], u)
                product(ps_u[:, 0:F], [xT[:, tb, h] for h in range(2)], w, KC, True, True).then_inc(s["u_mm"], 1)

            def turn_hidden(u, first=False):
                pe.wait_ge(s["hid_s"], u + 1)
                if not first:
                    pe.wait_ge(s["hidT_s"], u)
                for c, col in enumerate(FCOL):
                    ins = pe.transpose(turn_h[:, c, :], hid[:, col:col + P], ident[:, :])
                ins.then_inc(s["turned_h"], 1)

            def down_product(u, t, w, start, stop, first=False):
                pe.wait_ge(s["hidT_s"], u + 1)
                if start and not first:
                    pe.wait_ge(s["y_s"], t)
                ins = product(ps_y[:, :], [hidT[:, h] for h in range(2)], w, FC, start, stop)
                if stop:
                    ins.then_inc(s["y_mm"], 1)

            halfword = lambda w, j, n, at, m: w.bitcast(F16)[:, j * n + at:j * n + at + m]

            def shared_gu(w, half):
                def chunk(j, k):
                    at = (k % 2) * HALVES * F + half * F
                    return halfword(w[:, k // 2, :], j, GU, at, F)
                return chunk

            def shared_unit(half):
                return shared_gu(sg, half), shared_gu(su, half)

            def shared_down(half):
                return lambda j, c: halfword(sd[:, half, :], j, DN, c * D, D)

            def routed_unit(r):
                e = pe.value_load(job_e[0:1, bass.ds(r, 1)], min_val=0, max_val=E - 1)
                return (lambda j, k: wg16[:, e, j * GU + k * F:j * GU + (k + 1) * F],
                        lambda j, k: wu16[:, e, j * GU + k * F:j * GU + (k + 1) * F])

            def rank_tokens():
                pe.wait_ge(s["picked_s"], 1)
                flat = picked[:, :, :].rearrange("p t e -> p (t e)")
                pe.matmul(ps_rank[:, 0:P], tri[:, :], flat, start=True, stop=True).then_inc(s["route_mm"], 1)
                pe.matmul(ps_rank[:, P:2 * P], ones[:, :], flat, start=True, stop=True).then_inc(s["route_mm"], 1)

            def table_product(m, b, start=False, stop=False):
                pe.wait_ge(s["hot_s"], m + 1)
                pe.matmul(ps_acc[:, :], hot_p[:, b, :], hot_j[:, b].rearrange("p a j -> p (a j)"),
                          start=start, stop=stop).then_inc(s["route_mm"], 1)

            wg16, wu16, wd16 = (w[:, :, :].bitcast(F16) for w in (wg, wu, wd))
            pe.wait_ge(s["consts"], 1)
            for t in range(TPB):
                turn_x1(t)
            K, V, Q = 1, 2, 0
            for n in blocks:
                def before(step, *args):
                    if n:
                        step(n - 1, *args)

                def logit_steps(j):
                    if n >= 2:
                        if j:
                            gate((n - 2) * TPB + j - 1)
                        if j < TPB:
                            turn_x2((n - 2) * TPB + j)

                def norm_step(i):
                    if 0 <= i - 1 - NORM_STEP < SHARED_PIECES:
                        column_norms(i - 1 - NORM_STEP)

                def next_x(j):
                    if n + 1 < NB:
                        turn_x1((n + 1) * TPB + j)

                pe.wait_ge(s["lo1"], (n + 1) * TPB)
                project(n, 0, K)
                before(sum_heads, KC - 1)
                project(n, 0, V)
                norm_step(n * KC)
                logit_steps(0)
                project(n, 0, Q)
                project(n, 1, K)
                logit_steps(1)
                project(n, 1, V)
                sum_heads(n, 0)
                norm_step(n * KC + 1)
                logit_steps(2)
                before(expand)
                project(n, 1, Q)
                logit_steps(3)
                project(n, 2, K)
                logit_steps(4)
                next_x(0)
                project(n, 2, V)
                sum_heads(n, 1)
                norm_step(n * KC + 2)
                next_x(1)
                project(n, 2, Q)
                next_x(2)
                before(output, 0)
                project(n, 3, K)
                next_x(3)
                before(output, 1)
                project(n, 3, V)
                sum_heads(n, 2)
                norm_step(n * KC + 3)
                before(output, 2)
                project(n, 3, Q)
                if n == NB - 1:
                    turn_free()
                    turn_tile(0, 0, True)
                    turned.append((s["xT_s"], 1))
                before(output, 3)
            last_tiles = range((NB - 1) * TPB, NT)
            sum_heads(NB - 1, KC - 1)
            ring_use = lambda b: max(m for m in range(len(release)) if m % RING == b)
            before_last = range((NB - 2) * TPB, (NB - 1) * TPB)
            pe.wait_ge(s["split_s"], SHARED_PIECES)
            pe.wait_ge(*release[ring_use(0)])
            gate_w, up_w = shared_unit(0)
            turn_x2(before_last[0])
            gate_product(0, 0, 0, gate_w, True)
            gate(before_last[0])
            turn_x2(before_last[1])
            pe.wait_ge(*release[ring_use(3)])
            up_product(0, 0, up_w, True)
            pe.wait_ge(s["silu_s"], 1)
            pe.wait_ge(s["hid_s"], 1)
            expand(NB - 1)
            gate(before_last[1])
            turn_x2(before_last[2])
            output(NB - 1, 0)
            gate(before_last[2])
            turn_x2(before_last[3])
            output(NB - 1, 1)
            gate(before_last[3])
            turn_x2(last_tiles[0])
            output(NB - 1, 2)
            gate(last_tiles[0])
            turn_x2(last_tiles[1])
            output(NB - 1, 3)
            gate(last_tiles[1])
            turn_x2(last_tiles[2])
            gate_w, up_w = shared_unit(1)
            gate_product(1, 0, 0, gate_w)
            gate(last_tiles[2])
            pe.wait_ge(s["x2_s"], last_tiles[1] + 1)
            turn_hidden(0, True)
            turn_x2(last_tiles[3])
            pe.wait_ge(s["x2_s"], last_tiles[2] + 1)
            up_product(1, 0, up_w)
            gate(last_tiles[3])
            turn_tile(1, 1)
            down_product(0, 0, shared_down(0), True, False, True)

            for u in range(1, HALVES * NT):
                t, half = u // 2, u % 2
                t_next = (u + 1) // 2
                if u + 1 < HALVES * NT:
                    gate_w, up_w = shared_unit(1 - half)
                else:
                    pe.wait_ge(s["split_s"], len(pieces) - 1)
                    pe.wait_ge(s["tables_s"], 1)
                    gate_w, up_w = routed_unit(0)
                gate_product(u + 1, t_next, t_next % 2, gate_w)
                turn_hidden(u, u == 0)
                up_product(u + 1, t_next % 2, up_w)
                if half == 0 and t < NT - 1:
                    turn_tile(t + 1, (t + 1) % 2)
                elif half == 0:
                    turn_gathered(0, 0)
                elif t == NT - 1:
                    turn_gathered(1, 1)
                if norm_unit(u - 1) is not None:
                    column_norms(norm_unit(u - 1))
                if u == 4:
                    rank_tokens()
                for m in table_choices(u - 1):
                    table_product(m, m % 4, start=m == 0, stop=m == TOPK * NT - 1)
                down_product(u, t, shared_down(half), half == 0, half == 1, t == 0)

            def job_step(r, b, ahead=2):
                u = HALVES * NT + r
                if ahead >= 1:
                    gate_w, up_w = routed_unit(r + 1)
                    gate_product(u + 1, NT + r + 1, 1 - b, gate_w)
                turn_hidden(u)
                if ahead >= 1:
                    up_product(u + 1, 1 - b, up_w)
                if ahead >= 2:
                    turn_gathered(r + 2, b)
                e = pe.value_load(job_e[0:1, bass.ds(r, 1)], min_val=0, max_val=E - 1)
                down_product(u, NT + r, lambda j, c: wd16[:, e, j * DN + c * D:j * DN + (c + 1) * D], True, True)

            pe.wait_ge(s["split_s"], len(pieces))
            with pe.Fori(0, (JOBS - 3) // 2) as i:
                job_step(2 * i, 0)
                job_step(2 * i + 1, 1)
            job_step(JOBS - 3, 0)
            job_step(JOBS - 2, 1, ahead=1)
            job_step(JOBS - 1, 0, ahead=0)

        @block.sync
        def _(sp):
            def load_x(t):
                if t >= TPB:
                    sp.wait_ge(s["xn1"], t - 1)
                sp.dma_start(x_rows(t), xf[t * P:(t + 1) * P, :]).then_inc(x_loaded(t)[0], 16)

            def load_res(t):
                if t >= 2:
                    sp.wait_ge(s["x2_s"], t - 1)
                else:
                    sp.wait_ge(s["xn1"], TPB)
                sp.dma_start(x_res[:, t % 2, :], xf[t * P:(t + 1) * P, :]).then_inc(s[f"xr{t % 2}"], 16)

            def store_tile(t):
                sp.wait_ge(s["x2_s"], t + 1)
                if 2 <= t + 2 < NT:
                    load_res(t + 2)
                sp.dma_start(out[t * P:(t + 1) * P, :], x2[:, t % 2, :]).then_inc(s[f"x2_out{t % 2}"], 16)
                sp.wait_ge(s["xn2_s"], t + 1)
                sp.dma_start(xn2_d[t * P:(t + 1) * P, :], xn2[:, t % 2, :]).then_inc(s[f"xn2_out{t % 2}"], 16)

            def load_part(m):
                if m >= FREE_PARTS + 3:
                    sp.wait_ge(s["w_lo"], m - 2)
                rows = slice((m % KC) * P, (m % KC + 1) * P)
                src = w_qkv[rows, part_cols(m)] if m < QKV_PARTS else w_out[rows, :]
                sp.dma_start(raw(m), src).then_inc(raw_in(m)[0], 16)

            for t in range(TPB):
                load_x(t)
            for m in range(4):
                load_part(m)
            sp.dma_start(gw[:, :, :], gate_w.rearrange("(k p) e -> p k e", p=P)).then_inc(s["gw_in"], 16)
            for m in range(4, QKV_PARTS + 1):
                load_part(m)
            load_res(0)
            load_res(1)
            load_x(TPB)
            load_x(TPB + 1)
            def down_parts(w, src):
                full = (FC - 1) * P
                return [(w[:, 0:(FC - 1) * D].rearrange("p (c d) -> p c d", d=D),
                         src[0:full, :].rearrange("(c p) d -> p c d", p=P)),
                        (w[OVER:P, (FC - 1) * D:DN], src[full:F, :])]

            shared = [(w[:, :, :].rearrange("p h (k f) -> p (h k) f", f=HALVES * F),
                       src.rearrange("(k p) f -> p k f", p=P)) for w, src in ((sg, sw_gate), (su, sw_up))]
            for h in range(HALVES):
                shared += down_parts(sd[:, h, :], sw_down[h * F:(h + 1) * F, :])
            sp.wait_ge(s["over_0"], 1)
            for dst, src in shared:
                sp.dma_start(dst, src).then_inc(s["shared_in"], 16)
            for m in range(QKV_PARTS + 1, PARTS):
                load_part(m)
            for n in range(NB + 2):
                for j in (0, 1):
                    if n and n + 1 < NB:
                        load_x((n + 1) * TPB + j)
                for j in (2, 3):
                    if n >= 2:
                        store_tile((n - 2) * TPB + j)
                for j in (2, 3):
                    if n + 1 < NB:
                        load_x((n + 1) * TPB + j)
                for j in (0, 1):
                    if 1 <= n <= NB:
                        store_tile((n - 1) * TPB + j)
            sp.wait_ge(s["gate_mm"], NT)
            stores_done(sp)
            for e in range(E):
                if e:
                    sp.wait_ge(s["g_mm"], 3 * (e - 1) + 1)
                for dst, src in [(w[:, e, :].rearrange("p (k f) -> p k f", f=F),
                                  src[e].rearrange("(k p) f -> p k f", p=P)) for w, src in ((wg, w_gate), (wu, w_up))]\
                        + down_parts(wd[:, e, :], w_down[e]):
                    sp.dma_start(dst, src).then_inc(s[f"w{e}"], 16)
            for q in range(2):
                sp.wait_ge(s[f"yo{q}"], 16 * ((NT + JOBS - 1 - q) // 2 + 1))

        @block.gpsimd
        def _(pool):
            step = [0]

            def const(ins):
                step[0] += 1
                ins.then_inc(s["cst_a"], 1)
                pool.wait_ge(s["cst_a"], step[0])

            def band(ap, pattern, base, mult):
                const(pool.affine_select(out=ap, in_=ap, compare_op=ALU.is_ge, fill=0.0, base=base,
                                         pattern=pattern, channel_multiplier=mult))

            const(pool.memset(ident[:, :], 0.0))
            const(pool.affine_select(out=ident[:, :], in_=ident[:, :], compare_op=ALU.not_equal, fill=1.0,
                                     base=0, pattern=[[-1, P]], channel_multiplier=1))
            const(pool.memset(neg_half[:, :], -0.5))
            pool.nop().then_inc(s["consts"], 1)

            def rstd_of(mv, ve, rs, gate, value, got, done):
                pool.wait_ge(s[gate], value)
                pool.tensor_scalar(ve, mv, LN_EPS, None, ALU.add).then_inc(s[got], 1)
                pool.wait_ge(s[got], value)
                pool.tensor_tensor(rs, ve, neg_half[:, :], ALU.pow).then_inc(s[done], 1)

            def rstd_1(t):
                b = t % 2
                rstd_of(mean_var[:, b, 1:2], var_eps[:, b:b + 1], rstd[:, b:b + 1], "var1", t + 1, "veps1", "rstd1")

            def rstd_2(t):
                b = t % 2
                rstd_of(mean_var2[:, b, 1:2], var_eps2[:, b:b + 1], rstd2[:, b:b + 1], "var2", t + 1, "veps2",
                        "rstd2_s")

            for t in range(TPB):
                rstd_1(t)
            for g in range(P // DH):
                pool.dma_start(dec[g * DH:(g + 1) * DH, :], bass.AP(decay.tensor, g, [[0, DH], [P // DH, KC]]),
                               allow_slow_non_contiguous=True).then_inc(s["dec_in"], 16)
            for ap, pat in ((head_of, [[P, KC], [-DH, HEADS]]),):
                const(pool.memset(ap[:, :, :], 1.0))
                band(ap[:, :, :], pat, 0, 1)
                band(ap[:, :, :], [[-a, b] for a, b in pat], DH - 1, -1)
            for h in range(HALVES):
                pool.memset(sd[0:OVER, h, (FC - 1) * D:DN], 0.0)
            pool.memset(ones_h[:, :], 1.0).then_inc(s["over_0"], 1)
            const(pool.memset(of_head[:, :, :], 1.0))
            band(of_head[:, :, :], [[P, KC], [1, P]], 0, -DH)
            band(of_head[:, :, :], [[-P, KC], [-1, P]], DH - 1, DH)
            pool.nop().then_inc(s["consts"], 1)
            for n in range(NB + 2):
                for t in (2, 3):
                    if n >= 2:
                        rstd_2((n - 2) * TPB + t)
                if n + 1 < NB:
                    for t in range(TPB):
                        rstd_1((n + 1) * TPB + t)
                for t in (0, 1):
                    if 1 <= n <= NB:
                        rstd_2((n - 1) * TPB + t)
            pool.wait_ge(s["gate_mm"], NT)
            stores_done(pool)
            pool.memset(wd[0:OVER, :, (FC - 1) * D:DN], 0.0).then_inc(s["over_0"], 1)
            const(pool.memset(ones[:, :], 1.0))
            const(pool.memset(tri[:, :], 1.0))
            band(tri[:, :], [[1, P]], -1, -1)
            const(pool.memset(not_first[:, :, :], 1.0))
            const(pool.memset(not_first[:, :, 0:1], 0.0))
            for ap, pat, b0, mult in ((iota_e, [[1, E]], 0, 0), (iota_j, [[1, JW]], 0, 0),
                                      (iota_p, [[1, P]], 0, 0), (token_1, [[0, TOPK], [P, NT]], 1, 1),
                                      (spare, [[0, 1]], T + 1, 1)):
                const(pool.iota(ap[:], pattern=pat, base=b0, channel_multiplier=mult,
                                allow_small_or_imprecise_dtypes=True))
            pool.nop().then_inc(s["cst_b"], 1)
            def add_shared(t):
                pool.wait_ge(s["y_s"], t + 1)
                pool.dma_start(out[t * P:(t + 1) * P, :], y_job[:, t % 2, :], accum_op=ALU.add)\
                    .then_inc(s[f"yo{t % 2}"], 16)

            def gather(r, b, first=False):
                if not first:
                    pool.wait_ge(s[f"gin{b}"], 8 * (r - b))
                pool.tensor_copy(idx_in[:, b:b + 1], job_tok[:, bass.ds(r, 1)]).then_inc(s["idxg_s"], 1)
                seen, free = pool.to_reg(r + 1), pool.to_reg(NT + r - 1)
                pool.wait_ge(s["xn2_out0"], 8 * NT)
                pool.wait_ge(s["idxg_s"], seen)
                pool.wait_ge(s["turned_x"], free)
                pool.indirect_dma_start(x_job[:, b, :], None, xn2_d[:, :],
                                        bass.IndirectOffsetOnAxis(idx_in[:, b:b + 1], 0))\
                    .then_inc(s[f"gin{b}"], 16)

            def scatter(r, b):
                pool.wait_ge(s[f"yo{1 - b}"], 16 * (NT // 2) + 8 * (r + b))
                pool.tensor_copy(idx_out[:, b:b + 1], job_tok[:, bass.ds(r, 1)]).then_inc(s["idxs_s"], 1)
                seen, ready = pool.to_reg(r + 1), pool.to_reg(NT + r + 1)
                pool.wait_ge(s["x2_out0"], 8 * NT)
                pool.wait_ge(s["idxs_s"], seen)
                pool.wait_ge(s["y_s"], ready)
                pool.indirect_dma_start(out[:, :], bass.IndirectOffsetOnAxis(idx_out[:, b:b + 1], 0),
                                        y_job[:, b, :], None, compute_op=ALU.add).then_inc(s[f"yo{b}"], 16)

            def fold(m):
                half = pieces[m][3].shape[1] // 2
                pool.wait_ge(s["square_s"], m + 1)
                pool.tensor_tensor(squares[:, 0:half], squares[:, 0:half], squares[:, half:2 * half], ALU.add)\
                    .then_inc(s["fold_s"], 1)

            const(pool.memset(zeros[:, :], 0.0))
            spare_parts = [(ap, a) for ap in (out, xn2_d) for a in range(8)]
            AHEAD = 4
            for t in range(NT - AHEAD + 1):
                for u in (2 * t, 2 * t + 1):
                    if norm_unit(u) is not None:
                        fold(norm_unit(u))
                add_shared(t)
                for ap, a in spare_parts[2 * t:2 * t + 2]:
                    pool.dma_start(ap[T:ROWS, a * (D // 8):(a + 1) * (D // 8)], zeros[:, :])\
                        .then_inc(s["pad_out"], 16)
            pool.wait_ge(s["tables_s"], 1)
            pool.wait_ge(s["pad_out"], 16 * 16)
            for r in range(AHEAD):
                gather(r, r % 2, first=r < 2)
                if r < AHEAD - 1:
                    add_shared(NT - AHEAD + 1 + r)
            with pool.Fori(0, (JOBS - AHEAD) // 2) as i:
                for b in range(2):
                    gather(2 * i + b + AHEAD, b)
                    scatter(2 * i + b, b)
            gather(JOBS - 1, 0)
            for r in range(JOBS - AHEAD - 1, JOBS):
                scatter(r, r % 2)

        @block.scalar
        def _(act):
            def hi_x(t):
                act.wait_ge(s["turned1"], t + 1)
                if t >= 2 * TPB:
                    act.wait_ge(s["q_mm"], KC * (t // TPB - 1))
                n, j = t // TPB, t % TPB
                act.copy(xnT_h[:, n % 2, :, j * P:(j + 1) * P], turned_x(t)).then_inc(s["hi1"], 1)

            def hi_w(m):
                act.wait_ge(*raw_in(m))
                act.copy(part_of(m, wq_h, wo_h), raw(m)).then_inc(s["w_hi"], 1)

            def phi_parts(n, c, which):
                i = n * KC + c
                item = k_item if which == 0 else q_item
                act.wait_ge(s["k_mm" if which == 0 else "q_mm"], i + 1)
                if i:
                    act.wait_ge(s["phik_s" if which == 0 else "phiq_s"], i)
                z = ring[item(n, c) % RING]
                act.activation(exp_z[:, which, :], z[:, :], ACT.Exp)
                act.activation(relu_z[:, which, :], z[:, :], ACT.Relu)\
                    .then_inc(s["k_act" if which == 0 else "q_act"], 1)

            def hi_a(n, c):
                i = n * KC + c
                act.wait_ge(s["a_s"], i + 1)
                if n:
                    act.wait_ge(s["out_mm"], n * TPB)
                act.copy(at_h[:, c, :], num[:, n % 2, c, :]).then_inc(s["ah_s"], 1)

            def move_xn2T(t):
                act.wait_ge(s["turned2"], t + 1)
                if t:
                    act.wait_ge(s["gate_mm"], t)
                act.copy(xn2T_h[:, :, :], turn[:, :, :]).then_inc(s["xn2Th_s"], 1)

            def square(m):
                x, kind, h, w = pieces[m]
                if m == 0:
                    act.wait_ge(s["shared_in"], 16 * SHARED_DMAS)
                    act.wait_ge(s["over_0"], 1)
                elif x < E and kind == 0:
                    act.wait_ge(s[f"w{x}"], 16 * 4)
                elif x == 0 and kind == 2:
                    act.wait_ge(s["over_0"], 2)
                if m:
                    act.wait_ge(s["norm_mm"], m)
                act.activation(squares[:, 0:w.shape[1]], w, ACT.Square).then_inc(s["square_s"], 1)

            def upper(m):
                x, kind, h, w = pieces[m]
                act.wait_ge(s["set_s"], 1 if x == E else x + 2)
                if m == 0:
                    act.wait_ge(s["w_lo"], PARTS)
                if m:
                    act.wait_ge(s["split_s"], m)
                n = w.shape[1]
                act.activation(planes_of(n)[:, 0, :], w, ACT.Copy, scale=scale[:, x, kind:kind + 1])\
                    .then_inc(s["upper_s"], 1)

            for t in range(TPB):
                hi_x(t)
                hi_w(t)
            for m in range(TPB, QKV_PARTS):
                hi_w(m)
            act.wait_ge(s["dec_in"], 16 * (P // DH))
            act.activation(dec[:, :], dec[:, :], ACT.Exp, scale=-1.0).then_inc(s["dec_e"], 1)
            act.wait_ge(s["gw_in"], 16)
            act.copy(gw_h[:, :, :], gw[:, :, :]).then_inc(s["gw_h_s"], 1)

            def upper_xT(t, b):
                act.wait_ge(s["turned_x"], t + 1)
                act.activation(xT[:, b, 0], turn_x[:, :, :], ACT.Copy, scale=LN_SCALE).then_inc(s["xTh_s"], 1)

            def gate_silu(u, by, first=False):
                act.wait_ge(s["g_mm"], u + 1)
                if not first:
                    act.wait_ge(s["hid_s"], u)
                act.activation(silu[:, :], ps_g[:, 0:F], ACT.Silu, scale=by).then_inc(s["silu_s"], 1)

            def upper_hidT(u, first=False):
                act.wait_ge(s["turned_h"], u + 1)
                act.copy(hidT[:, 0], turn_h[:, 0:FC, :]).then_inc(s["hidTh_s"], 1)

            def move_y(t, b, first=False):
                act.wait_ge(s["y_mm"], t + 1)
                if not first:
                    act.wait_ge(s[f"yo{b}"], 8 * (t - b))
                act.activation(y_job[:, b, :], ps_y[:, :], ACT.Copy, scale=y_scale[:, E:E + 1])\
                    .then_inc(s["y_s"], 1)

            def load_job_x(t, b, first=False):
                act.wait_ge(*tile_sem("xn2_out", t))
                if not first:
                    act.wait_ge(s["turned_x"], t - 1)
                act.dma_start(x_job[:, b, :], xn2_d[bass.ds(t * P, P), :]).then_inc(s[f"xin{b}"], 16)

            def piece_step(i):
                if i < KC:
                    hi_w(QKV_PARTS + i)
                if 0 <= i - NORM_STEP < SHARED_PIECES:
                    square(i - NORM_STEP)
                if 0 <= i - SPLIT_STEP < SHARED_PIECES:
                    upper(i - SPLIT_STEP)

            for n in blocks:
                moves = [(n - 2) * TPB + j for j in range(TPB)] if n >= 2 else []
                phi_parts(n, 0, 0)
                for t in moves[0:1]:
                    move_xn2T(t)
                phi_parts(n, 0, 1)
                piece_step(n * KC)
                phi_parts(n, 1, 0)
                for t in moves[1:3]:
                    move_xn2T(t)
                if n:
                    for c in chunks:
                        hi_a(n - 1, c)
                phi_parts(n, 1, 1)
                for t in moves[3:4]:
                    move_xn2T(t)
                piece_step(n * KC + 1)
                phi_parts(n, 2, 0)

                def next_x(j):
                    if n + 1 < NB:
                        hi_x((n + 1) * TPB + j)

                next_x(0)
                next_x(1)
                phi_parts(n, 2, 1)
                next_x(2)
                piece_step(n * KC + 2)
                if n == NB - 1:
                    act.wait_ge(s["xn1"], NT)
                    load_job_x(0, 0, True)
                    load_job_x(1, 1, True)
                phi_parts(n, 3, 0)
                next_x(3)
                phi_parts(n, 3, 1)
                piece_step(n * KC + 3)
            shared_by = silu_scale[:, E:E + 1]
            first = (NB - 2) * TPB
            upper_xT(0, 0)
            move_xn2T(first)
            gate_silu(0, shared_by, True)
            move_xn2T(first + 1)
            for c in chunks:
                hi_a(NB - 1, c)
            for t in range(first + 2, NT - 1):
                move_xn2T(t)
            gate_silu(1, shared_by)
            upper_hidT(0)
            move_xn2T(NT - 1)
            upper_xT(1, 1)
            load_job_x(2, 0)
            load_job_x(3, 1)
            for u in range(1, HALVES * NT):
                t, half = u // 2, u % 2
                if u + 1 < HALVES * NT:
                    gate_silu(u + 1, shared_by)
                else:
                    act.wait_ge(s["tables_s"], 2)
                    gate_silu(u + 1, job_silu[:, 0:1])
                upper_hidT(u)
                if SPLIT_UNIT <= u < SPLIT_UNIT + 3 * E:
                    upper(SHARED_PIECES + u - SPLIT_UNIT)
                if half == 0:
                    upper_xT(t + 1, (t + 1) % 2)
                    if t + 3 < NT:
                        load_job_x(t + 3, (t + 3) % 2)
                elif t == NT - 1:
                    upper_xT(NT + 1, 1)
                if norm_unit(u) is not None:
                    square(norm_unit(u))
                if u == 2:
                    act.wait_ge(s["rt_exp_in"], 1)
                    act.activation(tab_a[:, :, :], tab_a[:, :, :], ACT.Exp).then_inc(s["rt_exp"], 1)
                if half == 1:
                    move_y(t, t % 2, first=t < 2)

            def job_step(r, b, ahead=2):
                u = HALVES * NT + r
                if ahead >= 1:
                    gate_silu(u + 1, job_silu[:, bass.ds(r + 1, 1)])
                upper_hidT(u)
                if ahead >= 2:
                    upper_xT(NT + r + 2, b)

            with act.Fori(0, (JOBS - 3) // 2) as i:
                job_step(2 * i, 0)
                job_step(2 * i + 1, 1)
            job_step(JOBS - 3, 0)
            job_step(JOBS - 2, 1, ahead=1)
            job_step(JOBS - 1, 0, ahead=0)

        @block.vector
        def _(dve):
            loc = [0]

            def link(ins):
                loc[0] += 1
                ins.then_inc(s["d_route"], 1)
                dve.wait_ge(s["d_route"], loc[0])

            def stats_x(t):
                b = t % 2
                dve.wait_ge(*x_loaded(t))
                if t >= 2:
                    dve.wait_ge(s["xn1"], t - 1)
                dve.bn_stats(stats[:, b, :], x_rows(t)).then_inc(s["stat1"], 1)
                dve.wait_ge(s["stat1"], t + 1)
                dve.bn_aggr(mean_var[:, b, :], stats[:, b, :]).then_inc(s["var1"], 1)

            def norm_x(t):
                b = t % 2
                dve.wait_ge(s["var1"], t + 1)
                dve.wait_ge(s["rstd1"], t + 1)
                if t:
                    dve.wait_ge(s["turned1"], t)
                dve.tensor_scalar(xn[:, :], x_rows(t), mean_var[:, b, 0:1], rstd[:, b:b + 1],
                                  ALU.subtract, ALU.mult).then_inc(s["xn1"], 1)

            def lo_x(t):
                n, j = t // TPB, t % TPB
                at = (slice(None), n % 2, slice(None), slice(j * P, (j + 1) * P))
                dve.wait_ge(s["hi1"], t + 1)
                dve.tensor_tensor(xnT_l[at], turned_x(t), xnT_h[at].bitcast(F32), ALU.subtract)\
                    .then_inc(s["lo1"], 1)

            def lo_w(m):
                dve.wait_ge(s["w_hi"], m + 1)
                dve.tensor_tensor(part_of(m, wq_l, wo_l), raw(m), part_of(m, wq_h, wo_h).bitcast(F32), ALU.subtract)\
                    .then_inc(s["w_lo"], 1)

            def states(n, c):
                i = n * KC + c
                dcol = dec[:, c:c + 1].broadcast_to([P, BLK])
                if i:
                    for name in ("kv_s", "sk_s", "skv_s", "qk_s", "num_s"):
                        dve.wait_ge(s[name], i)
                    dve.wait_ge(s["carry_s"], 2 * i)
                dve.wait_ge(s["k_act"], i + 1)
                dve.scalar_tensor_tensor(out=run_k[:, :], in0=exp_z[:, 0, :], scalar=1.0, in1=relu_z[:, 0, :],
                                         op0=ALU.min, op1=ALU.add).then_inc(s["phik_s"], 1)
                dve.wait_ge(s["phik_s"], i + 1)
                dve.wait_ge(s["v_mm"], i + 1)
                dve.tensor_tensor(run_kv[:, :], run_k[:, :], ring[v_item(n, c) % RING][:, :], ALU.mult)\
                    .then_inc(s["kv_s"], 1)
                start = n % BPS == 0
                if not start:
                    dve.wait_ge(s["carry_s"], 2 * (i - KC + 1))
                dve.tensor_tensor_scan(run_k[:, :], dcol, run_k[:, :], 0.0 if start else carry[:, 0, c:c + 1],
                                       ALU.mult, ALU.add).then_inc(s["sk_s"], 1)
                dve.wait_ge(s["kv_s"], i + 1)
                dve.tensor_tensor_scan(run_kv[:, :], dcol, run_kv[:, :], 0.0 if start else carry[:, 1, c:c + 1],
                                       ALU.mult, ALU.add).then_inc(s["skv_s"], 1)

            def query(n, c):
                i = n * KC + c
                dve.wait_ge(s["q_act"], i + 1)
                dve.scalar_tensor_tensor(out=phi_q[:, :], in0=exp_z[:, 1, :], scalar=1.0, in1=relu_z[:, 1, :],
                                         op0=ALU.min, op1=ALU.add).then_inc(s["phiq_s"], 1)
                dve.wait_ge(s["sk_s"], i + 1)
                dve.tensor_copy(carry[:, 0, c:c + 1], run_k[:, BLK - 1:BLK]).then_inc(s["carry_s"], 1)
                dve.wait_ge(s["phiq_s"], i + 1)
                if i >= 2:
                    dve.wait_ge(s["den_mm"], i - 1)
                dve.tensor_tensor(qk[:, c % 2, :], phi_q[:, :], run_k[:, :], ALU.mult).then_inc(s["qk_s"], 1)
                dve.wait_ge(s["skv_s"], i + 1)
                dve.tensor_copy(carry[:, 1, c:c + 1], run_kv[:, BLK - 1:BLK]).then_inc(s["carry_s"], 1)
                if n >= 2:
                    dve.wait_ge(s["out_mm"], (n - 1) * TPB)
                dve.tensor_tensor(num[:, n % 2, c, :], phi_q[:, :], run_kv[:, :], ALU.mult).then_inc(s["num_s"], 1)

            def denominators(n):
                dve.wait_ge(s["den_mm"], (n + 1) * KC)
                if n:
                    dve.wait_ge(s["ex_mm"], n * KC)
                dve.tensor_scalar(den[:, :], ps_den[0:HEADS, :], DEN_EPS, None, ALU.max).then_inc(s["den_max"], 1)
                dve.wait_ge(s["den_max"], n + 1)
                dve.reciprocal(den[:, :], den[:, :]).then_inc(s["rden_s"], 1)

            def divide(n):
                for c in chunks:
                    i = n * KC + c
                    dve.wait_ge(s["ex_mm"], i + 1)
                    dve.wait_ge(s["num_s"], i + 1)
                    a = num[:, n % 2, c, :]
                    dve.tensor_tensor(a, a, ring[items[(n, c, "ex")] % RING][:, :], ALU.mult).then_inc(s["a_s"], 1)

            def lo_a(n):
                for c in chunks:
                    i = n * KC + c
                    dve.wait_ge(s["ah_s"], i + 1)
                    a = num[:, n % 2, c, :]
                    dve.tensor_tensor(at_l[:, n % 2, c, :], a, at_h[:, c, :].bitcast(F32), ALU.subtract)\
                        .then_inc(s["al_s"], 1)

            def residual(t):
                b = t % 2
                dve.wait_ge(s["out_mm"], t + 1)
                dve.wait_ge(*tile_sem("xr", t))
                if t >= 2:
                    dve.wait_ge(s[f"x2_out{b}"], 16 * (t // 2))
                    dve.wait_ge(s["xn2_s"], t - 1)
                n, j = t // TPB, t % TPB
                dve.tensor_tensor(x2[:, b, :], ring[items[(n, j, "out")] % RING][:, :], x_res[:, b, :], ALU.add)\
                    .then_inc(s["x2_s"], 1)
                dve.wait_ge(s["x2_s"], t + 1)
                dve.bn_stats(stats2[:, b, :], x2[:, b, :]).then_inc(s["stat2"], 1)
                dve.wait_ge(s["stat2"], t + 1)
                dve.bn_aggr(mean_var2[:, b, :], stats2[:, b, :]).then_inc(s["var2"], 1)

            def lo_xn2T(t):
                dve.wait_ge(s["xn2Th_s"], t + 1)
                dve.tensor_tensor(xn2T_l[:, :, :], turn[:, :, :], xn2T_h[:, :, :].bitcast(F32), ALU.subtract)\
                    .then_inc(s["xn2T_s"], 1)

            def norm_2(t):
                b = t % 2
                dve.wait_ge(s["var2"], t + 1)
                dve.wait_ge(s["rstd2_s"], t + 1)
                if t >= 2:
                    dve.wait_ge(s[f"xn2_out{b}"], 16 * (t // 2))
                    dve.wait_ge(s["turned2"], t - 1)
                dve.tensor_scalar(xn2[:, b, :], x2[:, b, :], mean_var2[:, b, 0:1], rstd2[:, b:b + 1],
                                  ALU.subtract, ALU.mult).then_inc(s["xn2_s"], 1)

            def rest_hidT(u):
                dve.wait_ge(s["hidTh_s"], u + 1)
                dve.tensor_tensor(hidT[:, 1], turn_h[:, 0:FC, :], hidT[:, 0], ALU.subtract).then_inc(s["hidT_s"], 1)

            def rest_xT(t, b):
                dve.wait_ge(s["xTh_s"], t + 1)
                dve.scalar_tensor_tensor(out=xT[:, b, 1], in0=turn_x[:, :, :], scalar=LN_SCALE, in1=xT[:, b, 0],
                                         op0=ALU.mult, op1=ALU.subtract).then_inc(s["xT_s"], 1)

            def hidden(u, by, first=False):
                dve.wait_ge(s["silu_s"], u + 1)
                dve.wait_ge(s["u_mm"], u + 1)
                if not first:
                    dve.wait_ge(s["turned_h"], u)
                dve.scalar_tensor_tensor(out=hid[:, :], in0=ps_u[:, 0:F], scalar=by, in1=silu[:, :],
                                         op0=ALU.mult, op1=ALU.mult).then_inc(s["hid_s"], 1)

            setn = [0]

            def set_link(ins):
                setn[0] += 1
                ins.then_inc(s["d_set"], 1)
                dve.wait_ge(s["d_set"], setn[0])

            def fold(m):
                half = pieces[m][3].shape[1] // 2
                dve.wait_ge(s["square_s"], m + 1)
                dve.tensor_tensor(squares[:, 0:half], squares[:, 0:half], squares[:, half:2 * half], ALU.add)\
                    .then_inc(s["fold_s"], 1)

            def column_max(m):
                x, kind, h, w = pieces[m]
                to = part_max[:, kind, h:h + 1] if x == E else col_max[:, x, kind:kind + 1]
                dve.wait_ge(s["norm_mm"], m + 1)
                dve.tensor_reduce(to, norms_of(m), AX_X, ALU.max).then_inc(s["max_s"], 1)

            def set_scales(x, n):
                dve.wait_ge(s["max_s"], SHARED_PIECES + 3 * (n - 1))
                big, he, sc, un = col_max[:, x, :], half_exp[:, x, :], scale[:, x, :], unscale[:, x, :]
                bits = lambda ap: ap.bitcast(I32)
                if x == E:
                    set_link(dve.tensor_tensor(big, part_max[:, :, 0], part_max[:, :, 1], ALU.add))
                set_link(dve.tensor_scalar(big, big, 2.0 ** -120, None, ALU.max))
                set_link(dve.tensor_scalar(he, bits(big), 24, None, ALU.arith_shift_right))
                set_link(dve.tensor_scalar(bits(un), he, 50, None, ALU.add))
                set_link(dve.tensor_scalar(bits(un), bits(un), 1 << 23, None, ALU.mult))
                set_link(dve.tensor_scalar(bits(sc), bits(un), -1, (127 + 127) << 23, ALU.mult, ALU.add))
                dve.tensor_scalar(silu_scale[:, x:x + 1], un[:, 0:1], 1.0 / LN_SCALE, None, ALU.mult)
                dve.tensor_scalar(hid_scale[:, x:x + 1], sc[:, 0:1], HID_SCALE / LN_SCALE, None, ALU.mult)
                set_link(dve.tensor_scalar(y_scale[:, x:x + 1], un[:, 0:1], un[:, 1:2], 1.0 / HID_SCALE,
                                           ALU.mult, ALU.mult))
                dve.tensor_tensor(y_scale[:, x:x + 1], y_scale[:, x:x + 1], un[:, 2:3], ALU.mult)\
                    .then_inc(s["set_s"], 1)
                dve.wait_ge(s["set_s"], n)

            def split(m):
                x, kind, h, w = pieces[m]
                n = w.shape[1]
                both = planes_of(n)
                dve.wait_ge(s["upper_s"], m + 1)
                dve.scalar_tensor_tensor(out=both[:, 1, :], in0=w, scalar=scale[:, x, kind:kind + 1],
                                         in1=both[:, 0, :], op0=ALU.mult, op1=ALU.subtract).then_inc(s["rest_s"], 1)
                dve.wait_ge(s["rest_s"], m + 1)
                dve.tensor_copy(w.bitcast(F16), both.rearrange("p a n -> p (a n)")).then_inc(s["split_s"], 1)

            stats_x(0)
            stats_x(1)
            norm_x(0)
            stats_x(2)
            norm_x(1)
            stats_x(3)
            lo_w(0)
            norm_x(2)
            lo_x(0)
            norm_x(3)
            lo_x(1)
            lo_w(1)
            lo_w(2)
            lo_x(2)
            lo_w(3)
            lo_x(3)
            for m in range(TPB, QKV_PARTS):
                lo_w(m)
            dve.wait_ge(s["dec_e"], 1)
            dve.tensor_scalar(dec[:, :], dec[:, :], 1.0, None, ALU.add).then_inc(s["dec_1"], 1)
            dve.wait_ge(s["dec_1"], 1)
            dve.reciprocal(dec[:, :], dec[:, :]).then_inc(s["dec_ok"], 1)
            dve.wait_ge(s["dec_ok"], 1)
            dve.wait_ge(s["gw_h_s"], 1)
            dve.tensor_tensor(gw_l[:, :, :], gw[:, :, :], gw_h[:, :, :].bitcast(F32), ALU.subtract)\
                .then_inc(s["gw_l_s"], 1)
            for n in blocks:
                def before(step, *args):
                    if n:
                        step(n - 1, *args)

                def tile_before(step, j, ago=1):
                    if n >= ago:
                        step((n - ago) * TPB + j)

                def next_x(step, j):
                    if n + 1 < NB:
                        step((n + 1) * TPB + j)

                def max_step(i):
                    if i < KC:
                        lo_w(QKV_PARTS + i)
                    m = i - 1 - NORM_STEP
                    if 0 <= m < SHARED_PIECES:
                        column_max(m)
                    if 0 <= m + 1 < SHARED_PIECES:
                        fold(m + 1)
                    if m == SHARED_PIECES - 1:
                        set_scales(E, 1)

                def split_step(i):
                    if 0 <= i - SPLIT_STEP < SHARED_PIECES:
                        split(i - SPLIT_STEP)

                before(denominators)
                states(n, 0)
                tile_before(lo_xn2T, 0, 2)
                tile_before(norm_2, 2, 2)
                tile_before(residual, 3, 2)
                query(n, 0)
                max_step(n * KC)
                next_x(stats_x, 0)
                next_x(stats_x, 1)
                tile_before(lo_xn2T, 1, 2)
                tile_before(norm_2, 3, 2)
                states(n, 1)
                tile_before(lo_xn2T, 2, 2)
                next_x(norm_x, 0)
                before(divide)
                split_step(n * KC)
                tile_before(lo_xn2T, 3, 2)
                query(n, 1)
                max_step(n * KC + 1)
                before(lo_a)
                next_x(lo_x, 0)
                next_x(norm_x, 1)
                next_x(stats_x, 2)
                states(n, 2)
                next_x(lo_x, 1)
                next_x(norm_x, 2)
                next_x(stats_x, 3)
                next_x(lo_x, 2)
                next_x(norm_x, 3)
                split_step(n * KC + 1)
                query(n, 2)
                max_step(n * KC + 2)
                next_x(lo_x, 3)
                tile_before(residual, 0)
                states(n, 3)
                tile_before(norm_2, 0)
                tile_before(residual, 1)
                split_step(n * KC + 2)
                query(n, 3)
                if n == NB - 1:
                    rest_xT(0, 0)
                max_step(n * KC + 3)
                split_step(n * KC + 3)
                tile_before(norm_2, 1)
                tile_before(residual, 2)
            t = (NB - 2) * TPB
            lo_xn2T(t)
            denominators(NB - 1)
            hidden(0, hid_scale[:, E:E + 1], True)
            norm_2(t + 2)
            residual(t + 3)
            lo_xn2T(t + 1)
            divide(NB - 1)
            lo_a(NB - 1)
            lo_xn2T(t + 2)
            norm_2(t + 3)
            residual(t + 4)
            lo_xn2T(t + 3)
            norm_2(t + 4)
            residual(t + 5)
            for j in range(4, 2 * TPB):
                lo_xn2T(t + j)
                if j == 2 * TPB - 1:
                    hidden(1, hid_scale[:, E:E + 1])
                    rest_xT(1, 1)
                if j + 1 < 2 * TPB:
                    norm_2(t + j + 1)
                if j == 2 * TPB - 2:
                    rest_hidT(0)
                if j + 2 < 2 * TPB:
                    residual(t + j + 2)
            wide = lambda ap: ap.unsqueeze(2).broadcast_to([P, NT, E])

            def softmax_in():
                dve.wait_ge(s["gate_mm"], NT)
                dve.tensor_copy(logits[:, :, :].rearrange("p t e -> p (t e)"), ps_gate[:, 0:NT * E])\
                    .then_inc(s["logit_s"], 1)
                stores_done(dve)
                dve.wait_ge(s["logit_s"], 1)
                link(dve.tensor_reduce(row_a[:, :], logits[:, :, :], AX_X, ALU.max))
                dve.tensor_tensor(tab_a[:, :, :], logits[:, :, :], wide(row_a[:, :]), ALU.subtract)\
                    .then_inc(s["rt_exp_in"], 1)

            def softmax_out():
                dve.wait_ge(s["rt_exp"], 1)
                link(dve.tensor_reduce(row_a[:, :], tab_a[:, :, :], AX_X, ALU.add))
                link(dve.reciprocal(row_b[:, :], row_a[:, :]))
                link(dve.tensor_tensor(score[:, :, :], tab_a[:, :, :], wide(row_b[:, :]), ALU.mult))

            def best_two():
                for t in range(NT):
                    ins = dve.max(top[:, t, :], score[:, t, :])
                link(ins)

            def best_experts():
                for t in range(NT):
                    ins = dve.max_index(top_i[:, t, :], top[:, t, :], score[:, t, :])
                link(ins)

            def picks():
                dve.wait_ge(s["cst_b"], 1)
                link(dve.tensor_copy(choice_w[:, :, :], top[:, :, 0:TOPK].rearrange("p t k -> p k t")))
                link(dve.tensor_copy(choice_h[:, :, :], choice_w[:, :, :]))
                dve.tensor_tensor(choice_l[:, :, :], choice_w[:, :, :], choice_h[:, :, :].bitcast(F32), ALU.subtract)
                link(dve.tensor_copy(top_f[:, :, :], top_i[:, :, 0:TOPK].rearrange("p t k -> p k t")))
                over_t = iota_e[:, :].unsqueeze(1).broadcast_to([P, NT, E])
                for k in range(TOPK):
                    ins = dve.tensor_tensor(pick[:, k], wide(top_f[:, k, :]), over_t, ALU.is_equal)
                link(ins)
                dve.tensor_tensor(picked[:, :, :], pick[:, 0], pick[:, 1], ALU.add).then_inc(s["picked_s"], 1)

            def first_slots():
                dve.wait_ge(s["route_mm"], 2)
                totals = ps_rank[:, P:2 * P].rearrange("p (t e) -> p e t", e=E)
                link(dve.tensor_copy(count[:, :, :], totals))
                flat = lambda ap: ap.rearrange("p e t -> p (e t)")
                link(dve.tensor_tensor_scan(flat(upto[:, :, :]), flat(not_first[:, :, :]), flat(count[:, :, :]), 0.0,
                                            ALU.mult, ALU.add))
                link(dve.tensor_scalar(jobs_i[:, :], upto[:, :, NT - 1], float(P - 1), None, ALU.add))
                link(dve.tensor_scalar(jobs_i[:, :], jobs_i[:, :], 7, None, ALU.arith_shift_right))
                link(dve.tensor_copy(jobs_f[:, :], jobs_i[:, :]))
                link(dve.tensor_tensor_scan(jobs_end[:, :], ones[:, 0:E], jobs_f[:, :], 0.0, ALU.mult, ALU.add))
                link(dve.tensor_tensor(jobs_beg[:, :], jobs_end[:, :], jobs_f[:, :], ALU.subtract))
                link(dve.tensor_tensor(base[:, :, :], upto[:, :, :], count[:, :, :], ALU.subtract))
                link(dve.tensor_scalar(jobs_beg[:, :], jobs_beg[:, :], float(P), None, ALU.mult))
                link(dve.tensor_tensor(base[:, :, :], base[:, :, :],
                                       jobs_beg[:, :].unsqueeze(2).broadcast_to([P, E, NT]), ALU.add))

            def slots():
                ranks = ps_rank[:, 0:P].rearrange("p (t e) -> p t e", e=E)
                link(dve.tensor_tensor(slot_e[:, :, :], ranks, base[:, :, :].rearrange("p e t -> p t e"), ALU.add))
                for k in range(TOPK):
                    link(dve.tensor_tensor(tab_a[:, :, :], slot_e[:, :, :], pick[:, k], ALU.mult))
                    link(dve.tensor_reduce(slot_f[:, k, :], tab_a[:, :, :], AX_X, ALU.add))
                link(dve.tensor_copy(slot_i[:, :], slot_f[:, :, :].rearrange("p k t -> p (k t)")))
                link(dve.tensor_scalar(slot_ji[:, :], slot_i[:, :], 7, None, ALU.arith_shift_right))
                link(dve.tensor_scalar(slot_pi[:, :], slot_i[:, :], P - 1, None, ALU.bitwise_and))
                link(dve.tensor_copy(slot_j[:, :], slot_ji[:, :]))
                link(dve.tensor_copy(slot_p[:, :], slot_pi[:, :]))

            def job_experts():
                link(dve.tensor_tensor(past[:, :, :], iota_j[:, :].unsqueeze(2).broadcast_to([P, JW, E]),
                                       jobs_end[:, :].unsqueeze(1).broadcast_to([P, JW, E]), ALU.is_ge))
                link(dve.tensor_reduce(job_ef[:, :], past[:, :, :], AX_X, ALU.add))
                dve.tensor_scalar(job_ec[:, :], job_ef[:, :], float(E - 1), None, ALU.min)
                link(dve.tensor_scalar(job_e[:, :], job_ef[:, :], float(E - 1), None, ALU.min))

            token_m = token_1[:, :, :].rearrange("p k t -> p (k t)")
            weight_h = choice_h[:, :, :].rearrange("p k t -> p (k t)").bitcast(F32)
            weight_l = choice_l[:, :, :].rearrange("p k t -> p (k t)")

            def one_hots(m, b):
                at = bass.ds(m, 1)
                if m >= 4:
                    dve.wait_ge(s["route_mm"], 2 + m - 3)
                dve.tensor_scalar(hot_p[:, b, :], iota_p[:, :], slot_p[:, at], None, ALU.is_equal)
                dve.tensor_scalar(hot_j[:, b, 0, :], iota_j[:, :], slot_j[:, at], token_m[:, at],
                                  ALU.is_equal, ALU.mult)
                dve.tensor_scalar(hot_j[:, b, 1, :], iota_j[:, :], slot_j[:, at], weight_h[:, at],
                                  ALU.is_equal, ALU.mult)
                dve.tensor_scalar(hot_j[:, b, 2, :], iota_j[:, :], slot_j[:, at], weight_l[:, at],
                                  ALU.is_equal, ALU.mult).then_inc(s["hot_s"], 1)

            def tables():
                dve.wait_ge(s["route_mm"], 2 + TOPK * NT)
                link(dve.tensor_copy(job_tok1[:, :], ps_acc[:, 0:JW]))
                link(dve.tensor_copy(job_w[:, :], ps_acc[:, JW:2 * JW]))
                link(dve.tensor_tensor(job_w[:, :], job_w[:, :], ps_acc[:, 2 * JW:3 * JW], ALU.add))
                link(dve.tensor_scalar(job_pad[:, :], job_tok1[:, :], 0.0, spare[:, 0:1], ALU.is_equal, ALU.mult))
                dve.scalar_tensor_tensor(out=job_tok[:, :], in0=job_tok1[:, :], scalar=-1.0, in1=job_pad[:, :],
                                         op0=ALU.add, op1=ALU.add).then_inc(s["tables_s"], 1)
                dve.wait_ge(s["tables_s"], 1)

            def job_masks():
                link(dve.tensor_tensor(job_is[:, :, :], iota_e[:, :].unsqueeze(1).broadcast_to([P, JW, E]),
                                       job_ec[:, :].unsqueeze(2).broadcast_to([P, JW, E]), ALU.is_equal))

            def of_jobs(out_ap, values, done):
                dve.wait_ge(s["set_s"], E + 1)
                link(dve.tensor_tensor(past[:, :, :], job_is[:, :, :],
                                       values[:, 0:E].unsqueeze(1).broadcast_to([P, JW, E]), ALU.mult))
                dve.tensor_reduce(out_ap[:, :], past[:, :, :], AX_X, ALU.add).then_inc(s["tables_s"], 1)
                dve.wait_ge(s["tables_s"], done)

            def job_weights():
                of_jobs(job_y, y_scale, 4)
                dve.tensor_tensor(job_y[:, :], job_y[:, :], job_w[:, :], ALU.mult).then_inc(s["tables_s"], 1)
                dve.wait_ge(s["tables_s"], 5)

            def weigh_y(r, b):
                t = NT + r
                dve.wait_ge(s["y_mm"], t + 1)
                dve.wait_ge(s[f"yo{b}"], 8 * (t - b))
                dve.tensor_scalar(y_job[:, b, :], ps_y[:, :], job_y[:, bass.ds(r, 1)], None, ALU.mult)\
                    .then_inc(s["y_s"], 1)

            shared_by = hid_scale[:, E:E + 1]
            routing = {1: softmax_in, 2: lambda: (softmax_out(), best_two()), 3: lambda: (best_experts(), picks()),
                       4: first_slots, 5: slots, 6: job_experts,
                       2 * LAST_TABLE + 2: tables, 2 * LAST_TABLE + 3: job_masks,
                       HALVES * NT - 4: lambda: of_jobs(job_silu, silu_scale, 2),
                       HALVES * NT - 3: lambda: of_jobs(job_hid, hid_scale, 3),
                       HALVES * NT - 2: job_weights}
            for u in range(1, HALVES * NT):
                t, half = u // 2, u % 2
                rest_hidT(u)
                if u + 1 < HALVES * NT:
                    hidden(u + 1, shared_by)
                else:
                    hidden(u + 1, job_hid[:, 0:1])
                if half == 0:
                    rest_xT(t + 1, (t + 1) % 2)
                elif t == NT - 1:
                    rest_xT(NT + 1, 1)
                for m in table_choices(u):
                    one_hots(m, m % 4)
                if norm_unit(u - 1) is not None:
                    column_max(norm_unit(u - 1))
                for e in range(E):
                    if u == SPLIT_UNIT + 3 * e - 1:
                        set_scales(e, e + 2)
                if SPLIT_UNIT <= u < SPLIT_UNIT + 3 * E:
                    split(SHARED_PIECES + u - SPLIT_UNIT)
                if u in routing:
                    routing[u]()

            def job_step(r, b, ahead=2):
                rest_hidT(HALVES * NT + r)
                if ahead >= 1:
                    hidden(HALVES * NT + r + 1, job_hid[:, bass.ds(r + 1, 1)])
                if ahead >= 2:
                    rest_xT(NT + r + 2, b)
                weigh_y(r, b)

            with dve.Fori(0, (JOBS - 3) // 2) as i:
                job_step(2 * i, 0)
                job_step(2 * i + 1, 1)
            job_step(JOBS - 3, 0)
            job_step(JOBS - 2, 1, ahead=1)
            job_step(JOBS - 1, 0, ahead=0)

_INS = ['L0_attn_x', 'L0_attn_w_qkv', 'L0_attn_w_out', 'L0_attn_decay_param', 'L0_ffn_gate_w', 'L0_ffn_w_gate',
        'L0_ffn_w_up', 'L0_ffn_w_down', 'L0_ffn_sw_gate', 'L0_ffn_sw_up', 'L0_ffn_sw_down']


def kernel(**inputs):
    import numpy as _np
    import concourse.bacc as _bacc
    from concourse import mybir as _mybir
    from concourse.bass_utils import run_bass_kernel_spmd as _run

    nc = _bacc.Bacc("TRN2", target_bir_lowering=False, num_devices=1)
    arrays, args = {}, []
    for name in _INS:
        a = _np.ascontiguousarray(inputs[name])
        arrays[f"in_{name}_dram"] = a
        args.append(nc.dram_tensor(f"in_{name}_dram", a.shape, _mybir.dt.from_np(a.dtype), kind="ExternalInput").ap())
    B, S, D = inputs['L0_attn_x'].shape
    args.append(nc.dram_tensor("out_dram", (B * S + 128, D), _mybir.dt.float32, kind="ExternalOutput").ap())
    preln_decay_attention_moe(nc, *args)
    r = _run(nc, [arrays], core_ids=[0])
    return r.results[0]["out_dram"][:B * S].reshape(B, S, D)
```
